# Optimizing a Trainium2 kernel written in Bass

```python
import numpy as np
import jax
import jax.numpy as jnp

def _softmax(x, axis=-1):
    return jax.nn.softmax(x, axis=axis)

def _gelu(x):
    return jax.nn.gelu(x, approximate=True)

def _silu(x):
    return jax.nn.silu(x)

def _sigmoid(x):
    return jax.nn.sigmoid(x)

def _layernorm(x, axis=-1, eps=1e-05):
    m = jnp.mean(x, axis=axis, keepdims=True)
    v = jnp.var(x, axis=axis, keepdims=True)
    return (x - m) / jnp.sqrt(v + eps)

def _scatter_add(tgt, idx, src, axis=0):
    return tgt.at[idx].add(src)

def _segment_sum(src, seg, n):
    return jax.ops.segment_sum(src, seg, n)
kernel_name = 'mk_prb_d2_jaxref_r8_be8133'

def setup_inputs(seed: int=0):
    np.random.seed(seed)
    _w = jnp.asarray

    def _L0_attn_setup():
        import jax, jax.numpy as jnp
        import numpy as np
        B, N, C = (2, 256, 128)
        H = 16
        D = C // H
        key = jax.random.key(seed)
        ks = jax.random.split(key, 5)
        s = 0.02
        return {'x': jax.random.normal(ks[0], (B, N, C), dtype=jnp.float32), 'qkv_w': jax.random.normal(ks[1], (C, 3 * C), dtype=jnp.float32) * s, 'qkv_b': jax.random.normal(ks[2], (3 * C,), dtype=jnp.float32) * s, 'proj_w': jax.random.normal(ks[3], (C, C), dtype=jnp.float32) * s, 'proj_b': jax.random.normal(ks[4], (C,), dtype=jnp.float32) * s}
    _L0_attn_in = _L0_attn_setup()

    def _L0_ffn_setup():
        import jax, jax.numpy as jnp
        import numpy as np
        B, S, D, H, F = (4, 512, 128, 16, 512)
        CAP = 0.125
        ROPE_BASE = 10000.0

        def rmsnorm(x, g):
            return x * jax.lax.rsqrt(jnp.mean(x * x, -1, keepdims=True) + 1e-06) * g

        def rope(t, pos):
            hd = t.shape[-1]
            inv = 1.0 / ROPE_BASE ** (jnp.arange(0, hd, 2, dtype=jnp.float32) / hd)
            f = pos[:, None, :, None].astype(jnp.float32) * inv
            emb = jnp.concatenate([f, f], axis=-1)
            cos, sin = (jnp.cos(emb), jnp.sin(emb))
            rot = jnp.concatenate([-t[..., hd // 2:], t[..., :hd // 2]], axis=-1)
            return t * cos + rot * sin
        key = jax.random.key(seed)
        ks = jax.random.split(key, 9)
        scale = 0.02
        x = jax.random.normal(ks[0], (B, S, D), jnp.float32)
        causal = jnp.where(jnp.tril(jnp.ones((S, S), bool)), 0.0, -1000000000.0).astype(jnp.float32)
        attention_mask = jnp.broadcast_to(causal[None, None], (B, 1, S, S))
        position_ids = jnp.broadcast_to(jnp.arange(S, dtype=jnp.int32), (B, S))
        return {'x': x, 'attention_mask': attention_mask, 'position_ids': position_ids, 'router_w': jax.random.normal(ks[1], (D, 1), jnp.float32) * scale, 'router_b': jnp.zeros((1,), jnp.float32), 'wq': jax.random.normal(ks[2], (D, D), jnp.float32) * scale, 'wk': jax.random.normal(ks[3], (D, D), jnp.float32) * scale, 'wv': jax.random.normal(ks[4], (D, D), jnp.float32) * scale, 'wo': jax.random.normal(ks[5], (D, D), jnp.float32) * scale, 'w1': jax.random.normal(ks[6], (D, F), jnp.float32) * scale, 'w2': jax.random.normal(ks[7], (F, D), jnp.float32) * scale, 'ln1': jnp.ones((D,), jnp.float32), 'ln2': jnp.ones((D,), jnp.float32)}
    _L0_ffn_in = _L0_ffn_setup()

    def _L1_attn_setup():
        import jax, jax.numpy as jnp
        import numpy as np
        B, N, D = (2, 256, 128)
        H, FD, HD = (16, 16, 64)
        ENC = 64
        EPS = 1e-12
        RD = 4.0
        RRD = 2.0
        R2 = float(np.sqrt(2.0))

        def taylor_exp(x):
            x2 = (x[..., :, None] * x[..., None, :]).reshape(*x.shape[:-1], FD * FD) / R2
            return jnp.concatenate([jnp.ones_like(x[..., :1]), x / RRD, x2 / RD], axis=-1)
        key = jax.random.key(seed)
        ks = jax.random.split(key, 7)
        s = 1.0 / np.sqrt(D)
        x = jax.random.normal(ks[0], (B, N, D), dtype=jnp.float32)
        Wq = jax.random.normal(ks[1], (H * FD, D), dtype=jnp.float32) * s
        Wk = jax.random.normal(ks[2], (H * FD, D), dtype=jnp.float32) * s
        Wv = jax.random.normal(ks[3], (H * HD, D), dtype=jnp.float32) * s
        Wk_enc = jax.random.normal(ks[4], (H * FD, D), dtype=jnp.float32) * s
        Wv_enc = jax.random.normal(ks[5], (H * HD, D), dtype=jnp.float32) * s
        Wout = jax.random.normal(ks[6], (D, H * HD), dtype=jnp.float32) * s
        return {'x': x, 'Wq': Wq, 'Wk': Wk, 'Wv': Wv, 'Wk_enc': Wk_enc, 'Wv_enc': Wv_enc, 'Wout': Wout}
    _L1_attn_in = _L1_attn_setup()

    def _L1_ffn_setup():
        import jax, jax.numpy as jnp
        import numpy as np
        B, S, IN, OUT, E, R = (8, 512, 128, 128, 8, 8)
        LORA_ALPHA = 16
        SCALING = LORA_ALPHA / R
        key = jax.random.key(seed)
        k = jax.random.split(key, 6)
        x = jax.random.normal(k[0], (B, S, IN), dtype=jnp.float32)
        base_w = jax.random.normal(k[1], (OUT, IN), dtype=jnp.float32) * 0.02
        base_b = jnp.zeros((OUT,), dtype=jnp.float32)
        lora_A = jax.random.normal(k[2], (IN, R), dtype=jnp.float32) * 0.02
        lora_B = jax.random.normal(k[3], (E, R, OUT), dtype=jnp.float32) * 0.02
        router_w = jax.random.normal(k[4], (E, IN), dtype=jnp.float32) * 0.02
        router_b = jnp.zeros((E,), dtype=jnp.float32)
        return {'x': x, 'base_w': base_w, 'base_b': base_b, 'lora_A': lora_A, 'lora_B': lora_B, 'router_w': router_w, 'router_b': router_b}
    _L1_ffn_in = _L1_ffn_setup()
    _d = {'L0_attn_x': _L0_attn_in['x'], 'L0_attn_qkv_w': _L0_attn_in['qkv_w'], 'L0_attn_qkv_b': _L0_attn_in['qkv_b'], 'L0_attn_proj_w': _L0_attn_in['proj_w'], 'L0_attn_proj_b': _L0_attn_in['proj_b'], 'L0_ffn_attention_mask': _L0_ffn_in['attention_mask'], 'L0_ffn_position_ids': _L0_ffn_in['position_ids'], 'L0_ffn_router_w': _L0_ffn_in['router_w'], 'L0_ffn_router_b': _L0_ffn_in['router_b'], 'L0_ffn_wq': _L0_ffn_in['wq'], 'L0_ffn_wk': _L0_ffn_in['wk'], 'L0_ffn_wv': _L0_ffn_in['wv'], 'L0_ffn_wo': _L0_ffn_in['wo'], 'L0_ffn_w1': _L0_ffn_in['w1'], 'L0_ffn_w2': _L0_ffn_in['w2'], 'L0_ffn_ln1': _L0_ffn_in['ln1'], 'L0_ffn_ln2': _L0_ffn_in['ln2'], 'L1_attn_Wq': _L1_attn_in['Wq'], 'L1_attn_Wk': _L1_attn_in['Wk'], 'L1_attn_Wv': _L1_attn_in['Wv'], 'L1_attn_Wk_enc': _L1_attn_in['Wk_enc'], 'L1_attn_Wv_enc': _L1_attn_in['Wv_enc'], 'L1_attn_Wout': _L1_attn_in['Wout'], 'L1_ffn_base_w': _L1_ffn_in['base_w'], 'L1_ffn_base_b': _L1_ffn_in['base_b'], 'L1_ffn_lora_A': _L1_ffn_in['lora_A'], 'L1_ffn_lora_B': _L1_ffn_in['lora_B'], 'L1_ffn_router_w': _L1_ffn_in['router_w'], 'L1_ffn_router_b': _L1_ffn_in['router_b']}
    _x0 = _d['L0_attn_x']
    _d['L0_attn_x'] = jax.random.normal(jax.random.fold_in(jax.random.key(seed), 1), (8, 512, 128), dtype=_x0.dtype)
    del _x0
    return _d

def reference(L0_attn_x, L0_attn_qkv_w, L0_attn_qkv_b, L0_attn_proj_w, L0_attn_proj_b, L0_ffn_attention_mask, L0_ffn_position_ids, L0_ffn_router_w, L0_ffn_router_b, L0_ffn_wq, L0_ffn_wk, L0_ffn_wv, L0_ffn_wo, L0_ffn_w1, L0_ffn_w2, L0_ffn_ln1, L0_ffn_ln2, L1_attn_Wq, L1_attn_Wk, L1_attn_Wv, L1_attn_Wk_enc, L1_attn_Wv_enc, L1_attn_Wout, L1_ffn_base_w, L1_ffn_base_b, L1_ffn_lora_A, L1_ffn_lora_B, L1_ffn_router_w, L1_ffn_router_b):

    def _L0_attn_ref(x, qkv_w, qkv_b, proj_w, proj_b):
        import jax, jax.numpy as jnp
        import numpy as np
        B, N, C = (2, 256, 128)
        H = 16
        D = C // H
        b, n, c = x.shape
        scale = (c // H) ** (-0.5)
        qkv = x @ qkv_w + qkv_b
        qkv = qkv.reshape(b, n, 3, H, D)
        q, k, v = jnp.moveaxis(qkv, 2, 0)
        attn = jnp.einsum('bnhd,bmhd->bhnm', q, k) * scale
        attn = jax.nn.softmax(attn, axis=-1)
        out = jnp.einsum('bhnm,bmhd->bnhd', attn, v).reshape(b, n, c)
        out = out @ proj_w + proj_b
        return out

    def _L0_ffn_ref(x, attention_mask, position_ids, router_w, router_b, wq, wk, wv, wo, w1, w2, ln1, ln2):
        import jax, jax.numpy as jnp
        import numpy as np
        B, S, D, H, F = (4, 512, 128, 16, 512)
        CAP = 0.125
        ROPE_BASE = 10000.0

        def rmsnorm(x, g):
            return x * jax.lax.rsqrt(jnp.mean(x * x, -1, keepdims=True) + 1e-06) * g

        def rope(t, pos):
            hd = t.shape[-1]
            inv = 1.0 / ROPE_BASE ** (jnp.arange(0, hd, 2, dtype=jnp.float32) / hd)
            f = pos[:, None, :, None].astype(jnp.float32) * inv
            emb = jnp.concatenate([f, f], axis=-1)
            cos, sin = (jnp.cos(emb), jnp.sin(emb))
            rot = jnp.concatenate([-t[..., hd // 2:], t[..., :hd // 2]], axis=-1)
            return t * cos + rot * sin
        b, s, d = x.shape
        hd = d // H
        weights = (x @ router_w)[..., 0] + router_b[0]
        k = int(CAP * s)
        topv, topi = jax.lax.top_k(weights, k)
        thr = topv[:, -1]
        sel_mask = (weights > thr[:, None]).astype(x.dtype)
        kc = k - 1
        sel_idx = jnp.sort(topi[:, :kc], axis=1)
        bidx = jnp.arange(b)[:, None]
        x_sel = x[bidx, sel_idx]
        pos_sel = position_ids[bidx, sel_idx]
        w_sel = weights[bidx, sel_idx]
        m = attention_mask[:, 0]
        m_sel = m[bidx[:, :, None], sel_idx[:, :, None], sel_idx[:, None, :]]
        hn = rmsnorm(x_sel, ln1)

        def heads(t):
            return t.reshape(b, kc, H, hd).transpose(0, 2, 1, 3)
        q = rope(heads(hn @ wq), pos_sel)
        kk = rope(heads(hn @ wk), pos_sel)
        v = heads(hn @ wv)
        sc = jnp.einsum('bhqd,bhkd->bhqk', q, kk) / np.sqrt(hd).astype(np.float32)
        sc = sc + m_sel[:, None]
        a = jax.nn.softmax(sc, axis=-1)
        o = jnp.einsum('bhqk,bhkd->bhqd', a, v).transpose(0, 2, 1, 3).reshape(b, kc, d) @ wo
        x1 = x_sel + o
        x2 = x1 + jax.nn.gelu(rmsnorm(x1, ln2) @ w1) @ w2
        proc = x2 * w_sel[..., None]
        out = jnp.zeros_like(x).at[bidx, sel_idx].set(proc)
        return out + x * (1.0 - sel_mask)[..., None]

    def _L1_attn_ref(x, Wq, Wk, Wv, Wk_enc, Wv_enc, Wout):
        import jax, jax.numpy as jnp
        import numpy as np
        B, N, D = (2, 256, 128)
        H, FD, HD = (16, 16, 64)
        ENC = 64
        EPS = 1e-12
        RD = 4.0
        RRD = 2.0
        R2 = float(np.sqrt(2.0))

        def taylor_exp(x):
            x2 = (x[..., :, None] * x[..., None, :]).reshape(*x.shape[:-1], FD * FD) / R2
            return jnp.concatenate([jnp.ones_like(x[..., :1]), x / RRD, x2 / RD], axis=-1)
        b, n, _ = x.shape
        q = (x @ Wq.T).reshape(b, n, H, FD).transpose(0, 2, 1, 3)
        k = (x @ Wk.T).reshape(b, n, H, FD).transpose(0, 2, 1, 3)
        v = (x @ Wv.T).reshape(b, n, H, HD).transpose(0, 2, 1, 3)
        x_enc = x[:, :ENC]
        k_enc = (x_enc @ Wk_enc.T).reshape(b, ENC, H, FD).transpose(0, 2, 1, 3)
        v_enc = (x_enc @ Wv_enc.T).reshape(b, ENC, H, HD).transpose(0, 2, 1, 3)
        k_enc_f = taylor_exp(k_enc)
        q_f = taylor_exp(q)
        k_f = taylor_exp(k)
        A_qk = jnp.einsum('bhnd,bhmd->bhnm', q_f, k_f)
        A_qk = jnp.tril(A_qk)
        y1 = jnp.einsum('bhnm,bhme->bhne', A_qk, v)
        A_qk2 = jnp.einsum('bhnd,bhmd->bhnm', q_f, k_enc_f)
        y2 = jnp.einsum('bhnm,bhme->bhne', A_qk2, v_enc)
        k_state = k_enc_f.sum(axis=2, keepdims=True) + jnp.cumsum(k_f, axis=2)
        z = 1.0 / ((q_f * k_state).sum(axis=-1) + EPS)
        out = (y1 + y2) * z[..., None]
        out = out.transpose(0, 2, 1, 3).reshape(b, n, H * HD)
        return out @ Wout.T

    def _L1_ffn_ref(x, base_w, base_b, lora_A, lora_B, router_w, router_b):
        import jax, jax.numpy as jnp
        import numpy as np
        B, S, IN, OUT, E, R = (8, 512, 128, 128, 8, 8)
        LORA_ALPHA = 16
        SCALING = LORA_ALPHA / R
        result = jnp.einsum('bsd,od->bso', x, base_w) + base_b
        logits = jnp.einsum('bsd,ed->bse', x, router_w) + router_b
        gating = jax.nn.softmax(logits, axis=-1).astype(jnp.bfloat16)
        mid = jnp.einsum('bsd,dr->bsr', x, lora_A)
        lora_out = jnp.einsum('bsr,erd,bse->bsd', mid, lora_B, gating.astype(jnp.float32))
        return result + lora_out * SCALING
    x = L0_attn_x
    xn = _layernorm(x, axis=-1)
    x = x + _L0_attn_ref(xn, L0_attn_qkv_w, L0_attn_qkv_b, L0_attn_proj_w, L0_attn_proj_b) + _L0_ffn_ref(xn, L0_ffn_attention_mask, L0_ffn_position_ids, L0_ffn_router_w, L0_ffn_router_b, L0_ffn_wq, L0_ffn_wk, L0_ffn_wv, L0_ffn_wo, L0_ffn_w1, L0_ffn_w2, L0_ffn_ln1, L0_ffn_ln2)
    xn = _layernorm(x, axis=-1)
    x = x + _L1_attn_ref(xn, L1_attn_Wq, L1_attn_Wk, L1_attn_Wv, L1_attn_Wk_enc, L1_attn_Wv_enc, L1_attn_Wout) + _L1_ffn_ref(xn, L1_ffn_base_w, L1_ffn_base_b, L1_ffn_lora_A, L1_ffn_lora_B, L1_ffn_router_w, L1_ffn_router_b)
    return x

_drawn_inputs = setup_inputs


def setup_inputs(seed=0):
    import zlib

    import numpy as np

    out = dict(_drawn_inputs(seed))
    spreads = {'L0_ffn_ln1': (1.0, 0.6),
     'L0_ffn_ln2': (1.0, 0.6),
     'L1_ffn_base_b': (0.0, 0.1),
     'L1_ffn_router_b': (0.0, 0.8)}
    factors = {'L0_attn_qkv_w': 8.0,
     'L0_attn_qkv_b': 8.0,
     'L0_attn_proj_w': 8.0,
     'L0_attn_proj_b': 3.504,
     'L0_ffn_wq': 8.0,
     'L0_ffn_wk': 8.0,
     'L0_ffn_wv': 8.0,
     'L0_ffn_wo': 8.0,
     'L0_ffn_w1': 8.0,
     'L0_ffn_w2': 8.0,
     'L1_ffn_lora_A': 8.0,
     'L1_ffn_lora_B': 8.0,
     'L1_ffn_router_w': 8.0}
    for name, (base, spread) in spreads.items():
        noise = np.random.default_rng([zlib.crc32(name.encode()), seed]).standard_normal(out[name].shape)
        drawn = base * np.exp(spread * noise) if base else spread * noise
        out[name] = jnp.asarray(drawn.astype(out[name].dtype))
    for name, factor in factors.items():
        out[name] = (out[name] * factor).astype(out[name].dtype)
    return out
```

```python
import numpy as np

import concourse.bass as bass
from concourse import mybir
from contextlib import ExitStack

F32 = mybir.dt.float32
BF16 = mybir.dt.bfloat16
I32 = mybir.dt.int32
ALU = mybir.AluOpType
ACT = mybir.ActivationFunctionType
AX = mybir.AxisListType

B, S, D = 8, 512, 128
C = S // 128
H, HD0 = 16, 8
FD, HD1 = 16, 64
HG = 4
G = H // HG
TERMS = 6
ENC = 64
CAP = 63
SLOT = 64
PAIRS = B // 2
F = 512
MB = 4
E, R = 8, 8
NEG = -3.0e38
FMIN = -3.4028235e38
LN_EPS, RMS_EPS = 1e-5, 1e-6
SC0 = float(HD0) ** -0.5
XW = D + 10
KEYS = ENC + S
KPAD = 640
BLK_Q = [0, 64, 192, 320, 384]
BLK_N = [S - q for q in BLK_Q]
BLK_O = [sum(BLK_N[:j]) for j in range(5)]
PW = sum(BLK_N)


def columns(parts):
    at, out = 0, {}
    for name, n in parts:
        out[name] = (at, at + n)
        at += n
    return out, at


CONST, NCONST = columns([("ident", 128), ("iota", SLOT), ("head", H), ("keep", PW), ("token", B * C),
                         ("off", PAIRS), ("eps", 4)])
ROWS, NROWS = columns([("vb", D), ("projb", D), ("baseb", D), ("ln1", D), ("ln2", D), ("rb", E), ("mrb", 1),
                       ("qkb", 2)])
W0, NW0 = columns([("q", D), ("k", D), ("vr", D + 1), ("proj", D), ("mqkv", 3 * D), ("wo", D), ("w1", F),
                   ("w2", F)])
W1, NW1 = columns([("q", H * FD), ("k", H * FD), ("ke", H * FD), ("v", H * HD1), ("ve", H * HD1),
                   ("out", H * HD1), ("comb", D + E + R)])

AREA = {}
_at = 0
for _n, _w in [("ST", PAIRS * 512), ("MR", PAIRS * 512), ("MRT", PAIRS * 512), ("MS", PAIRS * SLOT),
               ("XS", PAIRS * XW), ("HN", PAIRS * D), ("HT", PAIRS * D), ("QKV", PAIRS * 3 * D),
               ("RQ", PAIRS * 2 * D), ("AB", 4 * D), ("QT", PAIRS * D), ("KBD", 2 * H * SLOT),
               ("AE", 2 * H * SLOT), ("AT", 2 * 8 * D), ("VBD", B * D)]:
    AREA[_n] = (_at, _at + _w)
    _at += _w
NAREA = max(_at, 8 * PW + G * 5 * 256)


def constants():
    c = np.zeros((128, NCONST), np.float32)
    p = np.arange(128)[:, None]

    def put(name, a):
        c[:, CONST[name][0]:CONST[name][1]] = a

    put("ident", np.eye(128))
    put("iota", np.arange(1, SLOT + 1)[None])
    put("head", p // HD0 == np.arange(H)[None])
    keep = np.zeros((128, PW), np.float32)
    for j in range(5):
        key = p + 128 * j - ENC
        q = BLK_Q[j] + np.arange(BLK_N[j])[None]
        keep[:, BLK_O[j]:BLK_O[j] + BLK_N[j]] = (key <= q) & (key < S)
    put("keep", keep)
    put("token", 128 * (np.arange(B * C) % C)[None] + p)
    put("off", S * np.minimum(2 * np.arange(PAIRS)[None] + p // SLOT, MB - 1))
    put("eps", np.array([LN_EPS, RMS_EPS, np.pi / 2, 1.0])[None])
    return c


def at(v, k, c):
    return v * k + c


def build(nc, x, consts, rows, w0, w1, lora_b, mask, pos, ones_rows, out):
    ctx = ExitStack()
    with ctx:
        def sb(name, shape, dt=F32):
            return ctx.enter_context(nc.sbuf_tensor(name, shape, dt))

        def sem(name):
            return ctx.enter_context(nc.semaphore(name))

        def dram(name, shape, dt=F32):
            return nc.dram_tensor(name, shape, dt, kind="Internal").ap()

        PS = ctx.enter_context(nc.psum_tensor("PS", [128, 8, 512], F32))
        X1 = sb("X1", [128, B * C, D])
        XN = sb("XN", [128, B * C, XW])
        cst = sb("cst", [128, NCONST])
        row = sb("row", [128, NROWS])
        w0s = sb("w0s", [128, NW0])
        w1s = sb("w1s", [128, NW1])
        lbs = sb("lbs", [E * R, D])
        QS = sb("QS", [128, G, HG, S], BF16)
        KS = sb("KS", [128, G, HG, KPAD], BF16)
        AR = sb("AR", [128, NAREA])
        PB = sb("PB", [128, 6800])
        st6 = sb("st6", [128, B * C, 6])
        mv = sb("mv", [128, B * C, 2])
        sm = sb("sm", [128, 8, B * C])
        WT = sb("WT", [128, B * C])

        def cc(name, t=cst, d=CONST):
            return t[:, d[name][0]:d[name][1]]

        ident = cc("ident")

        def rr(name):
            return cc(name, row, ROWS)

        def ww0(name):
            return cc(name, w0s, W0)

        def ww1(name):
            return cc(name, w1s, W1)

        def ar(name):
            return AR[:, AREA[name][0]:AREA[name][1]]

        sqk0 = dram("sqk0", (B, 2, 3, HD0, H, S), BF16)
        sv0 = dram("sv0", (B, G, 128, C * HG * 9))
        sw = dram("sw", (B * C, 128))
        sq1 = dram("sq1", (B, 3, FD, H, S), BF16)
        sk1 = dram("sk1", (B, 3, FD, H, KEYS), BF16)
        sx1 = dram("sx1", (B, 128, S))
        sz = dram("sz", (2, HG, S))

        xT0 = [PB[:, 512 * p:512 * p + 512] for p in range(2)]
        part0 = [PB[:, 1024 + 1536 * p:2560 + 1536 * p].bitcast(BF16).rearrange("p (q t n) -> p q t n", q=2, t=3)
                 for p in range(2)]
        rem0 = PB[:, 4096:5120].rearrange("p (q n) -> p q n", q=2)
        vb0 = [PB[:, 5120 + 576 * p:5696 + 576 * p].rearrange("p (g c h n) -> p g c h n", g=G, c=C, h=HG)
               for p in range(2)]
        wrow = PB[0:32, 6272:6400]
        P0 = AR[:, 0:8192].rearrange("p (u h n) -> p u h n", u=4, h=HG)
        V0 = AR[:, 8192:8192 + 576].rearrange("p (g c h n) -> p g c h n", g=G, c=C, h=HG)
        OS0 = PB[:, 0:512]
        OQ0 = PB[:, 512:1024].rearrange("p (c n) -> p c n", c=C)
        OT0 = PB[:, 1024:1536]
        mx = PB[:, 1536:1568].rearrange("p (s n) -> p s n", s=2)
        rd0 = PB[:, 1568:1584].rearrange("p (c h) -> p c h", c=C)
        mT = PB[0:16, 1600:1856].rearrange("p (s n) -> p s n", s=2)
        mR = PB[0:16, 1856:1984]
        mN = [PB[0:16, 2048 + 192 * p:2240 + 192 * p].bitcast(BF16).rearrange("p (t n) -> p t n", t=3)
              for p in range(2)]
        ST = ar("ST").rearrange("p (r c n) -> p r c n", r=PAIRS, c=C)
        MR = ar("MR").rearrange("p (r n) -> p r n", r=PAIRS)
        MRT = ar("MRT").rearrange("p (r c n) -> p r c n", r=PAIRS, c=C)
        MS = ar("MS").rearrange("p (r n) -> p r n", r=PAIRS)
        XS = ar("XS").rearrange("p (r n) -> p r n", r=PAIRS)
        HN = ar("HN").rearrange("p (r n) -> p r n", r=PAIRS)
        HT = ar("HT").rearrange("p (r n) -> p r n", r=PAIRS)
        QKV = ar("QKV").rearrange("p (r n) -> p r n", r=PAIRS)
        RQ = ar("RQ").rearrange("p (r n) -> p r n", r=PAIRS)
        AB = ar("AB").rearrange("p (a n) -> p a n", a=2)
        QT = ar("QT").rearrange("p (r n) -> p r n", r=PAIRS)
        KBD = ar("KBD").rearrange("p (s h n) -> p s h n", s=2, h=H)
        AE = ar("AE").rearrange("p (s h n) -> p s h n", s=2, h=H)
        AT = ar("AT").rearrange("p (s k n) -> p s k n", s=2, k=8)
        VBD = ar("VBD").rearrange("p (b k n) -> p b k n", b=B, k=8)
        GT = ar("MR").rearrange("p (r f n) -> p r f n", r=PAIRS, f=4)
        SS = ar("MRT").rearrange("p (r c n) -> p r c n", r=PAIRS, c=C)
        OO, OOT, X1S, H2 = (ar("KBD")[:, 512 * i:512 * i + 512].rearrange("p (r n) -> p r n", r=PAIRS)
                            for i in range(4))
        H2T, PR = (ar("RQ")[:, 512 * i:512 * i + 512].rearrange("p (r n) -> p r n", r=PAIRS) for i in range(2))
        RS = ar("QKV")[0:96, 0:512]
        SEL = ar("QKV")[0:B, 512:1536].rearrange("p (a n) -> p a n", a=2)
        m8 = sb("m8", [B, 16])
        TS = sb("TS", [128, C, 96])
        idx = sb("idx", [128, PAIRS], I32)
        posi = sb("posi", [128, MB * C], I32)
        ang = PB[:, 6400:6720].rearrange("p (a n) -> p a n", a=5)
        am = sb("am", [128, 3, PAIRS, H])
        xT1 = [PB[:, 512 * p:512 * p + 512] for p in range(2)]
        pq1 = AR[:, 0:3072].bitcast(BF16).rearrange("p (s t a n) -> p s t a n", s=2, t=3, a=2)
        pk1 = AR[:, 3072:3072 + 3456].bitcast(BF16).rearrange("p (s t a n) -> p s t a n", s=2, t=3, a=2)
        rem1 = AR[:, 6528:6528 + 2176].rearrange("p (a n) -> p a n", a=2)
        xb1 = [AR[:, 8704 + 512 * p:9216 + 512 * p].rearrange("p (c n) -> p c n", c=C) for p in range(2)]
        LG = PB[:, 1024:1024 + 96].rearrange("p (a c e) -> p a c e", a=3, c=C)
        lmx = PB[:, 1136:1136 + 16].rearrange("p (a c) -> p a c", a=4)
        GB = PB[:, 1152:1168].bitcast(BF16).rearrange("p (c e) -> p c e", c=C)
        GM = PB[:, 1280:1280 + 512].rearrange("p (s c n) -> p s c n", s=2, c=C)
        GTT = PB[0:64, 1792:2816].rearrange("p (s n) -> p s n", s=2)
        P1 = AR[:, 0:8 * PW].rearrange("p (s h n) -> p s h n", s=2, h=HG)
        V1 = AR[:, 8 * PW:8 * PW + G * 1280].rearrange("p (g j n) -> p g j n", g=G, j=5)
        Y1 = PB[:, 0:2048].rearrange("p (s a n) -> p s a n", s=2, a=2)
        Z1 = PB[:, 2048:4096].rearrange("p (s a n) -> p s a n", s=2, a=2)
        dn1 = PB[:, 4096:5120].rearrange("p (s n) -> p s n", s=2)
        xTc = PB[:, 5120:5632]
        dR = PB[:, 5632:5664].rearrange("p (s n) -> p s n", s=2)
        zR = PB[:, 5664:5696].rearrange("p (s n) -> p s n", s=2)

        names = """consts_in rows_in w0_in w1_in pos_in ones_in stats_done std_done rstd_done xn_done
            x1b_done xt_ps xt_sb qk_ps part1 rem_done part2 part3 v_ps v_sb wt_done wt_ps wt_row
            wrow_out wrow_in rs_done rs_ps ts_done onehot trig_r trig trig_done vzero g_ps xs_done
            idx_done mr_ps mrt_done ms_ps ms_done ssq_done hn_done ht_ps ht_sb mqkv_ps mqkv_sb
            rope_done rt_ps qt_done kbd_done sc_ps smx_done exp_mod ae_done at_ps at_sb vbd_done
            op_ps oo_done oot_ps oot_sb wo_ps x1s_done ssq2_done h2_done h2t_ps h2t_sb w1_ps
            gelu_done w2_ps pr_done ss_ps ss_sb scat_ps ffn_done mod_x1 chain_v chain_p ks_zero
            av_zero s_full s_free mt_ps mt_sb mn_done st_full exp_done av_done os_done ot_ps rd_done
            oq_done otT_ps otT_sb proj_ps x1_l0 xt2_ps xt2_sb q1_ps k1_ps p1_part1 p1_rem p1_part3
            cb_ps gm_done lexp gtr_ps gtr_sb lora_ps x1_l1 base_done lmax_done kpad v1_zero sf1 sq1d
            mask1 v1_ps v1_cp y_ps y_cp den_ps den_cp rec1 yn1 wout_ps out_add xb_done""".split()
        s = {n: sem(n) for n in names}
        x_in = [sem(f"x_in{r}") for r in range(PAIRS)]
        wr0 = [sem(f"wr0_{p}") for p in range(2)]
        wr1 = [sem(f"wr1_{p}") for p in range(2)]
        ld = [sem(f"ld{g}") for g in range(G)]
        ld1 = [sem(f"ld1_{g}") for g in range(G)]
        ext = [sem(f"ext{p}") for p in range(2)]
        mr_in = sem("mr_in")
        xt_in, den_in, z_out, z_in, outs = (sem(n) for n in ("xt_in", "den_in", "z_out", "z_in", "outs"))

        def bank(n):
            return PS[:, n, :]

        block = ctx.enter_context(nc.Block())

        def load_stacks(sp, g, d, q, k, n, done):
            heads = slice(HG * g, HG * g + HG)
            for first, part, times in ((0, 0, 3), (3, 1, 2), (5, 2, 1)):
                rows_ = slice(d * first, d * (first + times))
                src = q[part, :, heads].rearrange("d h n -> d (h n)")
                if times > 1:
                    src = src.unsqueeze(0).to_broadcast([times, d, HG * S])
                sp.dma_start(QS[rows_, g].rearrange("p h n -> p (h n)"), src).then_inc(done, 16)
                sp.dma_start(KS[rows_, g, :, 0:n], k[0:times, :, heads].rearrange("t d h n -> (t d) h n")).then_inc(done, 16)

        @block.sync
        def _(sp):
            sp.dma_start(cst[:], consts).then_inc(s["consts_in"], 16)
            for b in range(B):
                sp.dma_start(X1[:, C * b:C * b + C, :], x[b].rearrange("(c p) d -> p c d", p=128)).then_inc(x_in[b // 2], 16)
                if b == 0:
                    sp.dma_start(row[:], rows).then_inc(s["rows_in"], 16)
                    sp.dma_start(w0s[:], w0).then_inc(s["w0_in"], 16)
            sp.dma_start(posi[:], pos).then_inc(s["pos_in"], 16)
            sp.dma_start(w1s[:], w1).then_inc(s["w1_in"], 16)
            sp.dma_start(lbs[:], lora_b).then_inc(s["w1_in"], 16)
            sp.wait_ge(s["ks_zero"], 1)
            sp.dma_start(KS[96:99, :, :, :], ones_rows).then_inc(s["ones_in"], 16)
            for b in range(B):
                p = b % 2
                sp.wait_ge(s["part3"], 2 * b + 2)
                for k in range(2):
                    for t in range(3):
                        sp.dma_start(sqk0[b, k, t].rearrange("d h n -> h d n"), part0[p][:, k, t, :]).then_inc(wr0[p], 16)
                sp.wait_ge(s["v_sb"], b + 1)
                sp.dma_start(sv0[b].rearrange("g p n -> p g n"),
                             vb0[p].rearrange("p g c h n -> p g (c h n)")).then_inc(wr0[p], 16)
            sp.wait_ge(s["wt_row"], 1)
            sp.dma_start(sw, wrow).then_inc(s["wrow_out"], 16)
            sp.wait_ge(s["wrow_out"], 16)
            sp.dma_start(SEL[:, 0, :], sw.rearrange("(b c) n -> b (c n)", b=B)).then_inc(s["wrow_in"], 16)
            for p in range(2):
                sp.wait_ge(wr0[p], 16 * 7 * (B // 2))

            def load0(b, g, bp):
                if bp is not None:
                    sp.wait_ge(s["av_done"], at(bp, 16, 4 * (g + 1)))
                if isinstance(b, int):
                    qk, vv = sqk0[b], sv0[b]
                else:
                    qk = sqk0[bass.ds(b, 1)].rearrange("o q t d h n -> (o q) t d h n")
                    vv = sv0[bass.ds(b, 1)].rearrange("o g p n -> (o g) p n")
                load_stacks(sp, g, HD0, qk[0], qk[1], S, ld[g])
                sp.dma_start(V0[:, g].rearrange("p c h n -> p (c h n)"), vv[g]).then_inc(ld[g], 16)

            def ext0(n2, p, g):
                sp.wait_ge(s["mn_done"], n2 * 2 - (1 - p) if isinstance(n2, int) else n2 * 2 - (1 - p))
                for t in range(3):
                    sp.dma_start(QS[96 + t:97 + t, g, :, :].rearrange("o h (c n) -> o (h c) n", c=C),
                                 mN[p][:, t, :]).then_inc(ext[p], 16)

            def steps0(b, first=False, last=False):
                for g in range(G):
                    if not (last and g == 3):
                        ext0(at(b, 2, (g + 1) // 2 + 1), (g + 1) % 2, (g + 1) % G)
                    if not last:
                        load0(b + 1, g, b)

            sp.wait_ge(s["mod_x1"], B)
            sp.wait_ge(s["ks_zero"], 2)
            for g in range(G):
                load0(0, g, None)
            ext0(1, 0, 0)
            steps0(0, first=True)
            with sp.Fori(1, B - 1) as i:
                steps0(i)
            steps0(B - 1, last=True)

            for b in range(B):
                p = b % 2
                sp.wait_ge(s["xt2_sb"], b + 1)
                sp.dma_start(sx1[b], xT1[p]).then_inc(wr1[p], 16)
                sp.wait_ge(s["p1_part3"], 4 * b + 4)
                for dst, src in ((sq1, pq1), (sk1, pk1)):
                    for a in range(2):
                        for t in range(3):
                            sp.dma_start(dst[b, t, :, 8 * a:8 * a + 8].rearrange("d h n -> h d n"), src[:, p, t, a, :]
                                         ).then_inc(wr1[p], 16)
            for p in range(2):
                sp.wait_ge(wr1[p], 16 * 13 * (B // 2))

            def load1(b, g, bp):
                if bp is not None:
                    sp.wait_ge(s["sf1"], at(bp, 64, 16 * (g + 1)))
                q, k = (t[b] if isinstance(b, int) else t[bass.ds(b, 1)].rearrange("o t d h n -> (o t) d h n")
                        for t in (sq1, sk1))
                load_stacks(sp, g, FD, q, k, KEYS, ld1[g])

            def den_chain(n, p):
                sp.wait_ge(s["den_cp"], n + 1)
                sp.dma_start(dR[:, p, :], dn1[0:128:32, p, :]).then_inc(den_in, 16)
                sp.wait_ge(s["rec1"], n + 1)
                if not isinstance(n, int) or n >= 2:
                    sp.wait_ge(s["yn1"], n * 2 - 2)
                sp.dma_start(sz[p].rearrange("h (a n) -> (h a) n", n=16), zR[:, p, :]).then_inc(z_out, 16)
                sp.wait_ge(z_out, n * 16 + 16)
                for a in range(2):
                    for k in range(2):
                        sp.dma_start(Z1[64 * k:64 * k + 64, p, a, :],
                                     sz[p, 2 * a + k:2 * a + k + 1, :].to_broadcast([64, S])).then_inc(z_in, 16)

            def store(b, n):
                sp.wait_ge(s["out_add"], n)
                dst = out[b] if isinstance(b, int) else out[bass.ds(b, 1)].rearrange("o t d -> (o t) d")
                src = X1[:, C * b:C * b + C, :] if isinstance(b, int) else X1[:, bass.ds(b * C, C), :]
                sp.dma_start(dst.rearrange("(c p) d -> p c d", p=128), src).then_inc(outs, 16)

            def steps1(b, first=False, last=False):
                for g in range(G):
                    if not (first and g == 0):
                        den_chain(at(b, 4, g - 1), (g - 1) % 2)
                    if not last:
                        load1(b + 1, g, b)
                    if g == 2 and not first:
                        store(b - 1, b)

            sp.wait_ge(s["x1_l1"], B)
            sp.dma_start(xTc, sx1[0]).then_inc(xt_in, 16)
            for g in range(G):
                load1(0, g, None)
            steps1(0, first=True)
            with sp.Fori(1, B - 1) as i:
                steps1(i)
            steps1(B - 1, last=True)
            den_chain(B * G - 1, 1)
            store(B - 1, B)
            sp.wait_ge(outs, 16 * B)

        @block.tensor
        def _(pe):
            mm = nc.tensor.matmul

            def tr(o, i, k):
                return nc.tensor.transpose(o, i, ident[0:k, 0:k])

            pe.wait_ge(s["consts_in"], 16)
            pe.wait_ge(s["w0_in"], 16)

            def prep0_a(b):
                pe.wait_ge(s["xn_done"], b + 1)
                if b >= 2:
                    pe.wait_ge(s["xt_sb"], b - 1)
                for c in range(C):
                    last = tr(bank(b % 2)[:, 128 * c:128 * c + 128], XN[:, C * b + c, 0:D], 128)
                last.then_inc(s["xt_ps"], 1)

            def prep0_b(b):
                p = b % 2
                pe.wait_ge(s["xt_sb"], b + 1)
                if b >= 2:
                    pe.wait_ge(s["rem_done"], 2 * b - 2)
                mm(bank(2 + 2 * p), ww0("q"), xT0[p], start=True, stop=True).then_inc(s["qk_ps"], 1)
                mm(bank(3 + 2 * p), ww0("k"), xT0[p], start=True, stop=True).then_inc(s["qk_ps"], 1)
                if b >= 1:
                    pe.wait_ge(s["v_sb"], b)
                    pe.wait_ge(s["wt_done"], b)
                for c in range(C):
                    o = 256 * (c % 2)
                    last = mm(PS[:, 6 + c // 2, o:o + D + 1], xT0[p][:, 128 * c:128 * c + 128], ww0("vr"),
                              start=True, stop=True)
                last.then_inc(s["v_ps"], 1)

            prep0_a(0)
            for b in range(B):
                if b + 1 < B:
                    prep0_a(b + 1)
                prep0_b(b)

            pe.wait_ge(s["wt_done"], B)
            tr(bank(0)[0:32, 0:128], WT[:], 128).then_inc(s["wt_ps"], 1)
            pe.wait_ge(s["rs_done"], 1)
            pe.wait_ge(s["rem_done"], 2 * B)
            for c in range(C):
                last = tr(bank(1)[:, 96 * c:96 * c + 96], RS[:, 128 * c:128 * c + 128], 96)
            last.then_inc(s["rs_ps"], 1)

            def halves(r):
                return [(2 * r + k, slice(64 * k, 64 * k + 64)) for k in range(2)]

            pe.wait_ge(s["trig_done"], 1)
            pe.wait_ge(s["v_sb"], B)
            for r in range(PAIRS):
                pe.wait_ge(s["onehot"], r + 1)
                if r == 0:
                    pe.wait_ge(s["wt_row"], 1)
                if r == 1:
                    pe.wait_ge(s["ts_done"], 1)
                for c in range(C):
                    for b, hs in halves(r):
                        last = mm(bank(r)[hs, 0:XW], ST[:, r, c, hs], XN[:, C * b + c, :], start=(c == 0),
                                  stop=(c == C - 1))
                last.then_inc(s["g_ps"], 1)
            for r in range(PAIRS):
                pe.wait_ge(s["hn_done"], r + 1)
                tr(bank(4 + r)[:, 0:128], HN[:, r, :], 128).then_inc(s["ht_ps"], 1)
            for r in range(PAIRS):
                pe.wait_ge(s["ht_sb"], r + 1)
                mm(bank(r)[:, 0:3 * D], HT[:, r, :], ww0("mqkv"), start=True, stop=True).then_inc(s["mqkv_ps"], 1)
            for r in range(PAIRS):
                pe.wait_ge(s["rope_done"], r + 1)
                tr(bank(4 + r)[:, 0:128], RQ[:, r, 0:D], 128)
                tr(bank(4 + r)[:, 128:256], RQ[:, r, D:2 * D], 128).then_inc(s["rt_ps"], 1)
            for r in range(PAIRS):
                pe.wait_ge(mr_in, 16 * PAIRS)
                for c in range(C):
                    last = tr(bank(r)[:, 128 * c:128 * c + 128], MR[:, r, 128 * c:128 * c + 128], 128)
                last.then_inc(s["mr_ps"], 1)
            for r in range(PAIRS):
                pe.wait_ge(s["mrt_done"], r + 1)
                if r == 0:
                    pe.wait_ge(s["qt_done"], PAIRS)
                for b, hs in halves(r):
                    for c in range(C):
                        last = mm(bank(r)[hs, 0:SLOT], MRT[:, r, c, hs], ST[:, r, c, hs],
                                  start=(c == 0), stop=(c == C - 1))
                last.then_inc(s["ms_ps"], 1)

            def scores(r):
                pe.wait_ge(s["ms_done"], PAIRS)
                if r == 2:
                    pe.wait_ge(s["smx_done"], 1)
                if r == 3:
                    pe.wait_ge(s["smx_done"], 2)
                for b, hs in halves(r):
                    pe.wait_ge(s["kbd_done"], b + 1)
                    for k in range(2):
                        last = mm(bank(2 * (r % 2) + k)[hs, :], QT[:, r, hs],
                                  KBD[:, b % 2, 8 * k:8 * k + 8, :].rearrange("p h n -> p (h n)"), start=True, stop=True)
                    last.then_inc(s["sc_ps"], 1)

            def att_t(r):
                pe.wait_ge(s["exp_mod"], r + 1)
                if r < 2:
                    pe.wait_ge(s["kbd_done"], 4 * r + 4)
                else:
                    pe.wait_ge(s["at_sb"], r - 1)
                for k in range(8):
                    o = 4 + 2 * (r % 2) + k // 4
                    last = tr(bank(o)[:, 128 * (k % 4):128 * (k % 4) + 128],
                              AE[:, r % 2, 2 * k:2 * k + 2, :].rearrange("p h n -> p (h n)"), 128)
                last.then_inc(s["at_ps"], 1)

            def att_v(r):
                pe.wait_ge(s["at_sb"], r + 1)
                pe.wait_ge(s["vbd_done"], 2 * r + 2)
                for k in range(8):
                    for b, hs in halves(r):
                        last = mm(bank(r)[hs, 16 * k:16 * k + 16], AT[:, r % 2, k, hs], VBD[:, b, k, :],
                                  start=(k == 0), stop=(k == 7), skip_group_check=True)
                last.then_inc(s["op_ps"], 1)

            scores(0)
            scores(1)
            att_t(0)
            scores(2)
            att_t(1)
            scores(3)
            pe.wait_ge(s["smx_done"], PAIRS)
            att_v(0)
            att_t(2)
            att_v(1)
            att_t(3)
            att_v(2)
            att_v(3)
            for r in range(PAIRS):
                pe.wait_ge(s["oo_done"], r + 1)
                tr(bank(4 + r)[:, 0:128], OO[:, r, :], 128).then_inc(s["oot_ps"], 1)
            for r in range(PAIRS):
                pe.wait_ge(s["oot_sb"], r + 1)
                mm(bank(r)[:, 0:128], OOT[:, r, :], ww0("wo"), start=True, stop=True).then_inc(s["wo_ps"], 1)
            for r in range(PAIRS):
                pe.wait_ge(s["oot_sb"], PAIRS)
                for c in range(C):
                    last = tr(bank(4 + r)[:, 128 * c:128 * c + 128], ST[:, r, c, :], 128)
                last.then_inc(s["ss_ps"], 1)
            for r in range(PAIRS):
                pe.wait_ge(s["h2_done"], r + 1)
                tr(bank(r)[:, 128:256], H2[:, r, :], 128).then_inc(s["h2t_ps"], 1)
            for r in range(PAIRS):
                pe.wait_ge(s["h2t_sb"], r + 1)
                pe.wait_ge(s["ss_sb"], r + 1)
                for f in range(4):
                    last = mm(bank(4 + r)[:, 128 * f:128 * f + 128], ww0("w1")[:, 128 * f:128 * f + 128], H2T[:, r, :],
                              start=True, stop=True)
                last.then_inc(s["w1_ps"], 1)
            for r in range(PAIRS):
                pe.wait_ge(s["gelu_done"], r + 1)
                for f in range(4):
                    last = mm(bank(r)[:, 256:384], GT[:, r, f, :], ww0("w2")[:, 128 * f:128 * f + 128], start=(f == 0),
                              stop=(f == 3))
                last.then_inc(s["w2_ps"], 1)
            for b in range(B):
                r, hs = b // 2, slice(64 * (b % 2), 64 * (b % 2) + 64)
                pe.wait_ge(s["pr_done"], r + 1)
                if b >= 4:
                    pe.wait_ge(s["ffn_done"], b - 3)
                for c in range(C):
                    last = mm(bank(4 + b % 4)[:, 128 * c:128 * c + 128], SS[hs, r, c, :], PR[hs, r, :], start=True,
                              stop=True)
                last.then_inc(s["scat_ps"], 1)

            def s_pass(n, g, h, halves_=(0, 1)):
                for k in halves_:
                    pe.wait_ge(s["s_free"], n * 2 + k - 1) if not isinstance(n, int) or 2 * n + k - 1 > 0 else None
                    for j in range(2):
                        q = 2 * k + j
                        last = mm(PS[:, 2 * k + j, :], QS[0:96, g, h, 128 * q:128 * q + 128], KS[0:96, g, h, 0:S],
                                  start=True, stop=True)
                    last.then_inc(s["s_full"], 1)

            def max_t(n, p):
                pe.wait_ge(s["s_free"], n * 8 + 8)
                tr(bank(7)[0:16, 0:128], mx[:, p, :], 128).then_inc(s["mt_ps"], 1)

            def st_pass(b, g, kc, heads):
                if kc == 0 and heads[0] == 0:
                    pe.wait_ge(ext[g % 2], at(b, 96, 48 * (g // 2 + 1)))
                for h in heads:
                    k = 16 * g + 4 * kc + h
                    if not isinstance(b, int) or b * 64 + k >= 2:
                        pe.wait_ge(s["exp_done"], at(b, 64, k - 1))
                    mm(bank(4 + k % 2), KS[0:99, g, h, 128 * kc:128 * kc + 128], QS[0:99, g, h, :], start=True,
                       stop=True).then_inc(s["st_full"], 1)

            def av(b, u, half, first=False):
                g, kc = u // 4, u % 4
                if half == 0:
                    pe.wait_ge(s["exp_done"], at(b, 64, 4 * u + 4))
                    if kc == 0 and not first:
                        pe.wait_ge(s["os_done"], at(b, 4, g))
                q = slice(256 * half, 256 * half + 256)
                for h in range(HG):
                    last = mm(PS[32 * h:32 * h + 9, 6, q], V0[:, g, kc, h, :], P0[:, u % 4, h, q],
                              start=(kc == 0 and half == 0), stop=(kc == C - 1), skip_group_check=True)
                if half == 1:
                    last.then_inc(s["av_done"], 1)

            def o_t(b, g):
                pe.wait_ge(s["os_done"], at(b, 4, g + 1))
                for c in range(C):
                    last = tr(bank(7)[:, 128 * c:128 * c + 128], OS0[:, 128 * c:128 * c + 128], 128)
                last.then_inc(s["ot_ps"], 1)

            def oq_t(b):
                pe.wait_ge(s["oq_done"], at(b, 4, 4))
                for c in range(C):
                    last = tr(bank(7)[:, 128 * c:128 * c + 128], OQ0[:, c, :], 128)
                last.then_inc(s["otT_ps"], 1)

            def proj(b):
                pe.wait_ge(s["otT_sb"], b + 1)
                for c in range(C):
                    last = mm(bank(7)[:, 128 * c:128 * c + 128], OT0[:, 128 * c:128 * c + 128], ww0("proj"),
                              start=True, stop=True)
                last.then_inc(s["proj_ps"], 1)

            def steps0(b, first=False, last=False):
                for u in range(16):
                    g, kc = u // 4, u % 4
                    if not (last and u >= 8):
                        u2 = (u + 8) % 16
                        nb = b if u < 8 else b + 1
                        if u2 % 4 == 0:
                            pe.wait_ge(ld[u2 // 4], at(nb, 112, 112))
                    st_pass(b, g, kc, (0, 1))
                    if not (last and u >= 8):
                        s_pass(at(nb, 16, u2), u2 // 4, u2 % 4, (0,))
                    before = (b, u - 2, first and u == 2) if u >= 2 else (b - 1, u + 14, False)
                    if u >= 2 or not first:
                        av(before[0], before[1], 0, before[2])
                    if kc == 0 and not (last and g == 3):
                        if not first or g > 1:
                            pe.wait_ge(s["oq_done"], at(b, 4, g - 1))
                        if first and g == 1:
                            pe.wait_ge(s["mt_sb"], 2)
                        max_t(at(b, 4, g + 1), (g + 1) % 2)
                    st_pass(b, g, kc, (2, 3))
                    if not (last and u >= 8):
                        s_pass(at(nb, 16, u2), u2 // 4, u2 % 4, (1,))
                    if u >= 2 or not first:
                        av(before[0], before[1], 1)
                    if kc == 2 and not (first and g == 0):
                        pe.wait_ge(s["mt_sb"], at(b, 4, g + 2) if not (last and g == 3) else 32)
                        if g == 1 and not first:
                            pe.wait_ge(s["x1_l0"], b)
                        if last and g == 3:
                            pe.wait_ge(s["oq_done"], 4 * B - 2)
                        if g == 0:
                            o_t(b - 1, 3)
                        else:
                            o_t(b, g - 1)
                    if u == 4 and not first:
                        pe.wait_ge(s["mt_sb"], at(b, 4, 3))
                        oq_t(b - 1)
                    if u == 5 and not first:
                        proj(b - 1)

            pe.wait_ge(s["ks_zero"], 2)
            pe.wait_ge(s["av_zero"], 1)
            pe.wait_ge(s["ones_in"], 16)
            pe.wait_ge(s["ffn_done"], B)
            for h in range(8):
                if h % 4 == 0:
                    pe.wait_ge(ld[h // 4], 112)
                s_pass(h, h // 4, h % 4)
            max_t(0, 0)
            pe.wait_ge(s["mt_sb"], 1)
            steps0(0, first=True)
            with pe.Fori(1, B - 1) as i:
                steps0(i)
            steps0(B - 1, last=True)
            for u in (14, 15):
                for half in range(2):
                    av(B - 1, u, half)
            pe.wait_ge(s["oq_done"], 4 * B - 1)
            o_t(B - 1, 3)
            oq_t(B - 1)
            proj(B - 1)

            pe.wait_ge(s["w1_in"], 32)
            pe.wait_ge(s["x1_l0"], B)

            def prep1_a(b):
                pe.wait_ge(s["xb_done"], b + 1)
                if b >= 2:
                    pe.wait_ge(s["xt2_sb"], b - 1)
                for c in range(C):
                    last = tr(bank(b % 2)[:, 128 * c:128 * c + 128], xb1[b % 2][:, c, :], 128)
                last.then_inc(s["xt2_ps"], 1)

            def prep1_b(b):
                p = b % 2
                pe.wait_ge(s["xt2_sb"], b + 1)
                for a in range(2):
                    if b or a:
                        pe.wait_ge(s["p1_rem"], 4 * b + 2 * a)
                    f = slice(128 * a, 128 * a + 128)
                    mm(bank(2), ww1("q")[:, f], xT1[p], start=True, stop=True).then_inc(s["q1_ps"], 1)
                    mm(bank(3), ww1("k")[:, f], xT1[p], start=True, stop=True)
                    mm(bank(4)[:, 0:128], ww1("ke")[:, f], xT1[p][:, 0:128], start=True, stop=True).then_inc(s["k1_ps"], 1)
                if b:
                    pe.wait_ge(s["gm_done"], b)
                for c in range(C):
                    o = 256 * (c % 2)
                    last = mm(PS[:, 5 + c // 2, o:o + D + E + R], xT1[p][:, 128 * c:128 * c + 128], ww1("comb"),
                              start=True, stop=True)
                last.then_inc(s["cb_ps"], 1)

            def prep1_c(b):
                p = b % 2
                pe.wait_ge(s["gm_done"], b + 1)
                if b:
                    pe.wait_ge(s["x1_l1"], b)
                for c in range(C):
                    last = tr(bank(7)[0:64, 128 * c:128 * c + 128], GM[:, p, c, :], 128)
                last.then_inc(s["gtr_ps"], 1)
                pe.wait_ge(s["gtr_sb"], b + 1)
                for c in range(C):
                    last = mm(bank(7)[:, 128 * c:128 * c + 128], GTT[:, p, 128 * c:128 * c + 128], lbs[:], start=True,
                              stop=True)
                last.then_inc(s["lora_ps"], 1)

            prep1_a(0)
            for b in range(B):
                if b + 1 < B:
                    prep1_a(b + 1)
                prep1_b(b)
                if b:
                    prep1_c(b - 1)
            prep1_c(B - 1)

            ones32 = cc("eps")[:, 3:4]

            def st1(b, g, h, half):
                if h == 0 and half == 0:
                    pe.wait_ge(ld1[g], at(b, 96, 96))
                for k, blocks in list(enumerate(((0,), (1,), (2, 3), (4,))))[2 * half:2 * half + 2]:
                    n = 16 * g + 4 * h + k
                    m = 4 * h + k
                    if not isinstance(b, int) or 64 * b + n >= 3:
                        pe.wait_ge(s["sq1d"], at(b, 64, n - 2 if m else n))
                    o = 0
                    for j in blocks:
                        last = mm(bank(m % 3)[:, o:o + BLK_N[j]], KS[0:96, g, h, 128 * j:128 * j + 128],
                                  QS[0:96, g, h, BLK_Q[j]:S], start=True, stop=True)
                        o += BLK_N[j]
                    last.then_inc(s["sf1"], 1)

            def av1(b, g, a, blocks):
                if a == 0 and blocks[0] == 0:
                    pe.wait_ge(s["mask1"], at(b, 16, 4 * g + 4))
                    pe.wait_ge(s["v1_cp"], at(b, 12, 3 * g + 3))
                if blocks[0] == 0 and not (isinstance(b, int) and b == 0 and g == 0):
                    pe.wait_ge(s["y_cp"], at(b, 8, 2 * g + a - 1))
                for j in blocks:
                    for k in range(2):
                        h = 2 * a + k
                        last = mm(PS[64 * k:64 * k + 64, 3 + a, BLK_Q[j]:S], V1[:, g, j, 64 * h:64 * h + 64],
                                  P1[:, g % 2, h, BLK_O[j]:BLK_O[j] + BLK_N[j]], start=(j == 0), stop=(j == 4))
                if blocks[-1] == 4:
                    last.then_inc(s["y_ps"], 1)

            def den1(b, g, blocks):
                if blocks[0] == 0 and not (isinstance(b, int) and b == 0 and g == 0):
                    pe.wait_ge(s["den_cp"], at(b, 4, g))
                for j in blocks:
                    for h in range(HG):
                        last = mm(PS[32 * h:32 * h + 1, 5, BLK_Q[j]:S], ones32,
                                  P1[:, g % 2, h, BLK_O[j]:BLK_O[j] + BLK_N[j]], start=(j == 0), stop=(j == 4))
                if blocks[-1] == 4:
                    last.then_inc(s["den_ps"], 1)

            def v1(b, g, fills):
                if g == 0 and fills[0] == 0:
                    pe.wait_ge(xt_in, at(b, 16, 16))
                f = slice(256 * g, 256 * g + 256)
                for k in fills:
                    if not (isinstance(b, int) and b == 0 and g == 0 and k == 0):
                        pe.wait_ge(s["v1_cp"], at(b, 12, 3 * g + k))
                    if k == 0:
                        mm(PS[0:64, 6, 0:256], xTc[:, 0:64], ww1("ve")[:, f], start=True, stop=True)
                        mm(PS[64:128, 6, 0:256], xTc[:, 0:64], ww1("v")[:, f], start=True, stop=True)
                        last = mm(PS[:, 6, 256:512], xTc[:, 64:192], ww1("v")[:, f], start=True, stop=True)
                    elif k == 1:
                        mm(PS[:, 6, 0:256], xTc[:, 192:320], ww1("v")[:, f], start=True, stop=True)
                        last = mm(PS[:, 6, 256:512], xTc[:, 320:448], ww1("v")[:, f], start=True, stop=True)
                    else:
                        last = mm(PS[0:64, 6, 0:256], xTc[:, 448:512], ww1("v")[:, f], start=True, stop=True)
                    last.then_inc(s["v1_ps"], 1)

            def wout(b, g, a):
                pe.wait_ge(s["yn1"], at(b, 8, 2 * g + a + 1))
                if a == 0 and g == 0 and not (isinstance(b, int) and b == 0):
                    pe.wait_ge(s["out_add"], b)
                for c in range(C):
                    k = 2 * g + a
                    last = mm(bank(7)[:, 128 * c:128 * c + 128], Y1[:, g % 2, a, 128 * c:128 * c + 128],
                              ww1("out")[:, 128 * k:128 * k + 128], start=(k == 0 and c == 0), stop=(k == 7),
                              skip_group_check=True)
                if a == 1:
                    last.then_inc(s["wout_ps"], 1)

            def prev(b, g, k):
                return (b, g - k) if g >= k else (b - 1, g - k + G)

            def steps1(b, first=False, last=False):
                for g in range(G):
                    before = not (first and g == 0)
                    p1 = prev(b, g, 1) if before else None
                    vn = (b if g < 3 else b + 1, (g + 1) % G) if not (last and g == 3) else None
                    out_of = prev(b, g, 3) if not (first and g < 3) else None
                    for a in range(2):
                        st1(b, g, 0, a)
                        if out_of:
                            wout(*out_of, a)
                    for a in range(2):
                        st1(b, g, 1 + a, 0)
                        if before:
                            av1(*p1, a, (0, 1))
                        st1(b, g, 1 + a, 1)
                        if before:
                            av1(*p1, a, (2, 3, 4))
                        if vn:
                            v1(*vn, (a,))
                    st1(b, g, 3, 0)
                    if before:
                        den1(*p1, (0, 1))
                    if vn:
                        v1(*vn, (2,))
                    st1(b, g, 3, 1)
                    if before:
                        den1(*p1, (2, 3, 4))

            pe.wait_ge(s["kpad"], 1)
            pe.wait_ge(s["v1_zero"], 1)
            pe.wait_ge(s["x1_l1"], B)
            v1(0, 0, (0, 1, 2))
            steps1(0, first=True)
            with pe.Fori(1, B - 1) as i:
                steps1(i)
            steps1(B - 1, last=True)
            every = (0, 1, 2, 3, 4)
            for a in range(2):
                wout(B - 1, 1, a)
            pe.wait_ge(s["mask1"], 16 * B)
            den1(B - 1, 3, every)
            av1(B - 1, 3, 0, every)
            av1(B - 1, 3, 1, every)
            for g in (2, 3):
                for a in range(2):
                    wout(B - 1, g, a)

        @block.scalar
        def _(act):
            A = nc.scalar.activation
            act.wait_ge(s["consts_in"], 16)
            act.wait_ge(s["stats_done"], 1)
            A(sm[:, 0, :], mv[:, :, 1], ACT.Sqrt, bias=cc("eps")[:, 0:1]).then_inc(s["std_done"], 1)
            act.wait_ge(s["rows_in"], 16)

            def xt0_copy(b):
                act.wait_ge(s["xt_ps"], b + 1)
                if b >= 2:
                    act.wait_ge(s["v_ps"], b - 1)
                A(xT0[b % 2], bank(b % 2), ACT.Copy).then_inc(s["xt_sb"], 1)

            xt0_copy(0)
            for b in range(B):
                p = b % 2
                if b >= 2:
                    act.wait_ge(wr0[p], 16 * 7 * (b // 2))
                for k in range(2):
                    act.wait_ge(s["qk_ps"], 2 * b + k + 1)
                    A(part0[p][:, k, 0, :], bank(2 + 2 * p + k), ACT.Identity, bias=rr("qkb")[:, k:k + 1]).then_inc(s["part1"], 1)
                if b + 1 < B:
                    xt0_copy(b + 1)
                for k in range(2):
                    act.wait_ge(s["rem_done"], 2 * b + k + 1)
                    A(part0[p][:, k, 1, :], rem0[:, k, :], ACT.Copy).then_inc(s["part2"], 1)
            act.wait_ge(s["trig_r"], 1)
            A(ang[:, 2, :], ang[:, 0, :], ACT.Sin)
            A(ang[:, 3, :], ang[:, 1, :], ACT.Sin).then_inc(s["trig"], 1)
            for r in range(PAIRS):
                act.wait_ge(s["xs_done"], r + 1)
                A(HN[:, r, :], XS[:, r, 0:D], ACT.Square, accum_out=sm[:, 3, r:r + 1]).then_inc(s["ssq_done"], 1)
            act.wait_ge(s["ssq_done"], PAIRS)
            A(sm[:, 4, 0:PAIRS], sm[:, 3, 0:PAIRS], ACT.Sqrt, bias=cc("eps")[:, 1:2], scale=1.0 / D).then_inc(s["std_done"], 1)
            for r in range(PAIRS):
                act.wait_ge(s["mqkv_ps"], r + 1)
                A(QKV[:, r, :], bank(r)[:, 0:3 * D], ACT.Copy).then_inc(s["mqkv_sb"], 1)
            act.wait_ge(s["vzero"], 1)
            act.wait_ge(s["mqkv_sb"], PAIRS)
            for b in range(B):
                r, hs = b // 2, slice(64 * (b % 2), 64 * (b % 2) + 64)
                v = QKV[hs, r, 2 * D:3 * D].rearrange("p (k o n) -> p k o n", k=8, o=2)
                A(VBD[0:64, b, :, 0:8], v[:, :, 0, :], ACT.Copy)
                A(VBD[64:128, b, :, 8:16], v[:, :, 1, :], ACT.Copy).then_inc(s["vbd_done"], 1)

            def at_copy(r):
                act.wait_ge(s["at_ps"], r + 1)
                if r >= 2:
                    act.wait_ge(s["op_ps"], r - 1)
                o = 4 + 2 * (r % 2)
                A(AT[:, r % 2, :, :].rearrange("p k n -> p (k n)"), PS[:, o:o + 2, :].rearrange("p b n -> p (b n)"),
                  ACT.Copy).then_inc(s["at_sb"], 1)

            for r in range(PAIRS):
                act.wait_ge(s["smx_done"], r + 1)
                act.wait_ge(s["ae_done"], r + 1)
                a = AE[:, r % 2, :, 0:CAP]
                A(a, a, ACT.Exp).then_inc(s["exp_mod"], 1)
                if r >= 1:
                    at_copy(r - 1)
            at_copy(PAIRS - 1)
            for r in range(PAIRS):
                act.wait_ge(s["oot_ps"], r + 1)
                A(OOT[:, r, :], bank(4 + r)[:, 0:128], ACT.Copy).then_inc(s["oot_sb"], 1)
            for r in range(PAIRS):
                act.wait_ge(s["ss_ps"], r + 1)
                A(SS[:, r, :, :].rearrange("p c n -> p (c n)"), bank(4 + r), ACT.Copy).then_inc(s["ss_sb"], 1)
            for r in range(PAIRS):
                act.wait_ge(s["x1s_done"], r + 1)
                A(H2[:, r, :], X1S[:, r, :], ACT.Square, accum_out=sm[:, 5, r:r + 1]).then_inc(s["ssq2_done"], 1)
            act.wait_ge(s["ssq2_done"], PAIRS)
            A(sm[:, 6, 0:PAIRS], sm[:, 5, 0:PAIRS], ACT.Sqrt, bias=cc("eps")[:, 1:2], scale=1.0 / D).then_inc(s["std_done"], 1)
            for r in range(PAIRS):
                act.wait_ge(s["h2t_ps"], r + 1)
                A(H2T[:, r, :], bank(r)[:, 128:256], ACT.Copy).then_inc(s["h2t_sb"], 1)
            for r in range(PAIRS):
                act.wait_ge(s["w1_ps"], r + 1)
                A(GT[:, r, :, :].rearrange("p f n -> p (f n)"), bank(4 + r), ACT.Gelu_apprx_tanh).then_inc(s["gelu_done"], 1)

            def os_copy(b, g, first=False):
                act.wait_ge(s["av_done"], at(b, 16, 4 * g + 4))
                if not first:
                    act.wait_ge(s["ot_ps"], at(b, 4, g))
                A(OS0, bank(6), ACT.Copy).then_inc(s["os_done"], 1)

            def steps0(b, first=False, last=False):
                for u in range(16):
                    if not (first and u < 4):
                        act.wait_ge(s["av_done"], at(b, 16, u - 3))
                    if u % 4 == 2 and not (first and u == 2):
                        if u == 2:
                            os_copy(b - 1, 3)
                        else:
                            os_copy(b, u // 4 - 1, first=first and u == 6)
                    for h in range(HG):
                        k = 4 * u + h
                        act.wait_ge(s["st_full"], at(b, 64, k + 1))
                        A(P0[:, u % 4, h, :], bank(4 + k % 2), ACT.Exp, scale=SC0).then_inc(s["exp_done"], 1)

            act.wait_ge(s["mod_x1"], B)
            steps0(0, first=True)
            with act.Fori(1, B - 1) as i:
                steps0(i)
            steps0(B - 1, last=True)
            os_copy(B - 1, 3)

            act.wait_ge(s["stats_done"], 2)
            A(sm[:, 0, :], mv[:, :, 1], ACT.Sqrt, bias=cc("eps")[:, 0:1]).then_inc(s["std_done"], 1)

            def gate_copy(b):
                act.wait_ge(s["gtr_ps"], b + 1)
                A(GTT[:, b % 2, :], bank(7)[0:64, :], ACT.Copy).then_inc(s["gtr_sb"], 1)

            for b in range(B):
                p = b % 2
                act.wait_ge(s["xt2_ps"], b + 1)
                if b >= 2:
                    act.wait_ge(wr1[p], 16 * 13 * (b // 2))
                    act.wait_ge(s["cb_ps"], b - 1)
                A(xT1[p], bank(p), ACT.Copy).then_inc(s["xt2_sb"], 1)
                for a in range(2):
                    m = 4 * b + 2 * a
                    act.wait_ge(s["q1_ps"], 2 * b + a + 1)
                    A(pq1[:, p, 0, a, :], bank(2), ACT.Copy).then_inc(s["p1_part1"], 1)
                    act.wait_ge(s["k1_ps"], 2 * b + a + 1)
                    A(pk1[:, p, 0, a, 0:ENC], bank(4)[:, 0:ENC], ACT.Copy)
                    A(pk1[:, p, 0, a, ENC:KEYS], bank(3), ACT.Copy).then_inc(s["p1_part1"], 1)
                    for k, (t, n) in enumerate(((pq1, S), (pk1, KEYS))):
                        act.wait_ge(s["p1_rem"], m + k + 1)
                        A(t[:, p, 1, a, :], rem1[:, k, 0:n], ACT.Copy).then_inc(s["part2"], 1)
                act.wait_ge(s["lmax_done"], b + 1)
                A(LG[:, 1], LG[:, 0], ACT.Exp).then_inc(s["lexp"], 1)
                if b:
                    gate_copy(b - 1)
            gate_copy(B - 1)

            def sq(b, g, h, first=False):
                if h == 0 and not (first and g < 2):
                    act.wait_ge(s["den_ps"], at(b, 4, g - 1))
                for k, (o, n) in enumerate(((BLK_O[0], BLK_N[0]), (BLK_O[1], BLK_N[1]), (BLK_O[2], BLK_N[2] + BLK_N[3]),
                                            (BLK_O[4], BLK_N[4]))):
                    m = 16 * g + 4 * h + k
                    act.wait_ge(s["sf1"], at(b, 64, m + 1))
                    A(P1[:, g % 2, h, o:o + n], bank((4 * h + k) % 3)[:, 0:n], ACT.Square, scale=0.25, bias=cc("eps")[:, 3:4]
                      ).then_inc(s["sq1d"], 1)

            def v_copy(b, g, k):
                act.wait_ge(s["v1_ps"], at(b, 12, 3 * g + k + 1))
                if k < 2:
                    A(V1[:, g, 2 * k:2 * k + 2, :].rearrange("p j n -> p (j n)"), bank(6), ACT.Copy).then_inc(s["v1_cp"], 1)
                else:
                    A(V1[0:64, g, 4, :], PS[0:64, 6, 0:256], ACT.Copy).then_inc(s["v1_cp"], 1)

            def steps1(b, first=False, last=False):
                for g in range(G):
                    for h in range(HG):
                        sq(b, g, h, first)
                        if h > 0 and not (last and g == 3):
                            v_copy(b if g < 3 else b + 1, (g + 1) % G, h - 1)
                    if g == 2 and not last:
                        nb = b + 1
                        src = sx1[nb] if isinstance(nb, int) else sx1[bass.ds(nb, 1)].rearrange("o p n -> (o p) n")
                        act.dma_start(xTc, src).then_inc(xt_in, 16)

            act.wait_ge(s["x1_l1"], B)
            for k in range(3):
                v_copy(0, 0, k)
            steps1(0, first=True)
            with act.Fori(1, B - 1) as i:
                steps1(i)
            steps1(B - 1, last=True)

        @block.vector
        def _(dve):
            v = nc.vector
            chain = [0]

            def link(ins):
                chain[0] += 1
                ins.then_inc(s["chain_v"], 1)
                dve.wait_ge(s["chain_v"], chain[0])

            def inv_sqrt(var, eps, scale, std, done, n):
                o = sm[:, 2, 0:n]
                t = sm[:, 7, 0:n]
                link(v.reciprocal(o, std))
                link(v.tensor_scalar(t, var, scale, eps, ALU.mult, ALU.add))
                link(v.tensor_tensor(t, t, o, ALU.mult))
                link(v.tensor_tensor(t, t, o, ALU.mult))
                link(v.tensor_scalar(t, t, -0.5, 1.5, ALU.mult, ALU.add))
                v.tensor_tensor(o, o, t, ALU.mult).then_inc(done, 1)

            for b in range(B):
                dve.wait_ge(x_in[b // 2], 32)
                for c in range(C):
                    ins = v.bn_stats(st6[:, C * b + c, :], X1[:, C * b + c, :])
                ins.then_inc(s["chain_v"], 1)
                chain[0] += 1
            dve.wait_ge(s["chain_v"], chain[0])
            for t in range(B * C):
                ins = v.bn_aggr(mv[:, t, :], st6[:, t, :])
            ins.then_inc(s["stats_done"], 1)
            dve.wait_ge(s["stats_done"], 1)
            dve.wait_ge(s["std_done"], 1)
            inv_sqrt(mv[:, :, 1], LN_EPS, 1.0, sm[:, 0, :], s["rstd_done"], B * C)
            dve.wait_ge(s["rstd_done"], 1)

            def norm0(b):
                for t in range(C * b, C * b + C):
                    ins = v.tensor_scalar(XN[:, t, 0:D], X1[:, t, :], mv[:, t, 0:1], sm[:, 2, t:t + 1], ALU.subtract, ALU.mult)
                ins.then_inc(s["xn_done"], 1)

            norm0(0)
            norm0(1)
            for p in range(2):
                link(v.memset(vb0[p].rearrange("p g c h n -> p (g c h n)"), 1.0))
            dve.wait_ge(s["rows_in"], 16)
            dve.wait_ge(s["pos_in"], 16)
            TWO_PI = 2 * np.pi
            C1, C2 = 6.28125, float(np.float32(0.0019350051879882812))
            C3 = TWO_PI - C1 - C2
            posf = sm[:, 1, 0:MB * C]
            link(v.tensor_copy(posf, posi[:]))
            inv = (np.float32(1.0) / np.float32(10000.0) ** (np.arange(0, HD0, 2, dtype=np.float32) / np.float32(HD0)))
            f4 = ang[:, 0, :].rearrange("p (n j) -> p n j", j=4)
            for j in range(4):
                link(v.tensor_scalar(f4[:, :, j], posf, float(inv[j]), None, ALU.mult))
            MAGIC = 12582912.0
            link(v.tensor_scalar(ang[:, 1, :], ang[:, 0, :], 1.0 / TWO_PI, MAGIC, ALU.mult, ALU.add))
            link(v.tensor_scalar(ang[:, 1, :], ang[:, 1, :], MAGIC, None, ALU.subtract))
            for k in (C1, C2, C3):
                link(v.scalar_tensor_tensor(out=ang[:, 0, :], in0=ang[:, 1, :], scalar=-k, in1=ang[:, 0, :], op0=ALU.mult,
                                            op1=ALU.add))
            link(v.tensor_scalar(ang[:, 0, :], ang[:, 0, :], 3.1415925, -3.1415925, ALU.min, ALU.max))
            link(v.tensor_scalar(ang[:, 1, :], ang[:, 0, :], -1.0, None, ALU.mult))
            link(v.tensor_tensor(ang[:, 1, :], ang[:, 0, :], ang[:, 1, :], ALU.max))
            v.tensor_scalar(ang[:, 1, :], ang[:, 1, :], -1.0, float(np.pi / 2), ALU.mult, ALU.add).then_inc(s["trig_r"], 1)

            def vps():
                return PS[:, 6:8, :].rearrange("p b (c n) -> p (b c) n", c=2)

            for b in range(B):
                p = b % 2
                if b + 2 < B:
                    norm0(b + 2)
                dve.wait_ge(s["v_ps"], b + 1)
                if b >= 2:
                    dve.wait_ge(wr0[p], 16 * 7 * (b // 2))
                vv = rr("vb").rearrange("p (g h n) -> p g h n", g=G, h=HG)
                for g in range(G):
                    ins = v.tensor_tensor(vb0[p][:, g, :, :, 0:8],
                                          vps()[:, :, 32 * g:32 * g + 32].rearrange("p c (h n) -> p c h n", h=HG),
                                          vv[:, g].unsqueeze(1).to_broadcast([128, C, HG, 8]), ALU.add)
                ins.then_inc(s["v_sb"], 1)
                v.tensor_scalar(WT[:, C * b:C * b + C], vps()[:, :, D], rr("mrb"), None, ALU.add).then_inc(s["wt_done"], 1)
                for k in range(2):
                    dve.wait_ge(s["part1"], 2 * b + k + 1)
                    if b:
                        dve.wait_ge(s["part3"], 2 * b + k - 1)
                    v.scalar_tensor_tensor(out=rem0[:, k, :], in0=bank(2 + 2 * p + k), scalar=rr("qkb")[:, k:k + 1],
                                           in1=part0[p][:, k, 0, :], op0=ALU.add, op1=ALU.subtract).then_inc(s["rem_done"], 1)
            dve.wait_ge(s["wt_ps"], 1)
            v.tensor_copy(wrow, bank(0)[0:32, 0:128]).then_inc(s["wt_row"], 1)
            dve.wait_ge(s["trig"], 1)
            a4 = ang.rearrange("p a (b c j) -> p a b c j", b=MB, c=C)
            for b in range(B):
                m = min(b, MB - 1)
                v.tensor_copy(XN[:, C * b:C * b + C, D:D + 4], a4[:, 3, m])
                v.tensor_copy(XN[:, C * b:C * b + C, D + 4:D + 8], a4[:, 2, m])
            v.tensor_copy(XN[:, :, D + 8], WT[:])
            v.tensor_copy(XN[:, :, D + 9], cc("token")).then_inc(s["trig_done"], 1)

            link(v.memset(RS, 0.0))
            link(v.memset(m8[:], 0.0))
            dve.wait_ge(s["wrow_in"], 16)
            link(v.tensor_copy(SEL[:, 1, :], SEL[:, 0, :]))
            for k in range(8):
                link(v.max(m8[:, 0:8], SEL[:, 1, :]))
                if k == 7:
                    link(v.tensor_copy(m8[:, 8:9], m8[:, 7:8]))
                    link(v.memset(m8[:, 7:8], NEG))
                link(v.match_replace(out=SEL[:, 1, :], in_to_replace=m8[:, 0:8], in_values=SEL[:, 1, :], imm_value=NEG))
            link(v.tensor_scalar(RS[32:32 + B, :], SEL[:, 0, :], m8[:, 8:9], None, ALU.is_le))
            link(v.tensor_scalar(SEL[:, 1, :], SEL[:, 1, :], NEG, None, ALU.is_equal))
            link(v.tensor_tensor_scan(RS[0:B, :], SEL[:, 1, :], SEL[:, 1, :], 0.0, ALU.add, ALU.max))
            v.tensor_tensor(RS[0:B, :], RS[0:B, :], SEL[:, 1, :], ALU.mult).then_inc(s["rs_done"], 1)
            dve.wait_ge(s["rs_ps"], 1)
            v.tensor_copy(TS[:].rearrange("p c n -> p (c n)"), bank(1)[:, 0:96 * C]).then_inc(s["ts_done"], 1)
            dve.wait_ge(s["ts_done"], 1)
            for r in range(PAIRS):
                for c in range(C):
                    for k in range(2):
                        ins = v.tensor_scalar(ST[:, r, c, 64 * k:64 * k + 64], cc("iota"), TS[:, c, 2 * r + k:2 * r + k + 1],
                                              None, ALU.is_equal)
                ins.then_inc(s["onehot"], 1)
            link(v.memset(VBD.rearrange("p b k n -> p (b k n)"), 0.0))
            v.memset(AE.rearrange("p s h n -> p (s h n)"), 0.0).then_inc(s["vzero"], 1)
            for r in range(PAIRS):
                dve.wait_ge(s["g_ps"], r + 1)
                v.tensor_copy(XS[:, r, :], bank(r)[:, 0:XW]).then_inc(s["xs_done"], 1)
            dve.wait_ge(s["xs_done"], PAIRS)
            v.tensor_tensor(idx[:], XS[:, :, D + 9], cc("off"), ALU.add).then_inc(s["idx_done"], 1)
            dve.wait_ge(s["std_done"], 2)
            inv_sqrt(sm[:, 3, 0:PAIRS], RMS_EPS, 1.0 / D, sm[:, 4, 0:PAIRS], s["rstd_done"], PAIRS)
            dve.wait_ge(s["rstd_done"], 2)
            for r in range(PAIRS):
                v.scalar_tensor_tensor(out=HN[:, r, :], in0=XS[:, r, 0:D], scalar=sm[:, 2, r:r + 1], in1=rr("ln1"),
                                       op0=ALU.mult, op1=ALU.mult).then_inc(s["hn_done"], 1)
            for r in range(PAIRS):
                dve.wait_ge(s["ht_ps"], r + 1)
                v.tensor_copy(HT[:, r, :], bank(4 + r)[:, 0:128]).then_inc(s["ht_sb"], 1)
            for r in range(PAIRS):
                dve.wait_ge(s["mqkv_sb"], r + 1)
                qk = QKV[:, r, 0:2 * D].rearrange("p (h n) -> p h n", n=4)
                xc, xs_ = (AB[:, a, :].rearrange("p (h n) -> p h n", n=4) for a in range(2))
                cosb, sinb = (XS[:, r, D + 4 * a:D + 4 * a + 4].unsqueeze(1).to_broadcast([128, 4 * H, 4]) for a in range(2))
                if r:
                    dve.wait_ge(s["rope_done"], r)
                v.tensor_tensor(xc, qk, cosb, ALU.mult)
                link(v.tensor_tensor(xs_, qk, sinb, ALU.mult))
                xc2, xs2, o2 = (t.rearrange("p (h o n) -> p h o n", o=2, n=4)
                                for t in (AB[:, 0, :], AB[:, 1, :], RQ[:, r, :]))
                v.tensor_tensor(o2[:, :, 0, :], xc2[:, :, 0, :], xs2[:, :, 1, :], ALU.subtract)
                v.tensor_tensor(o2[:, :, 1, :], xc2[:, :, 1, :], xs2[:, :, 0, :], ALU.add).then_inc(s["rope_done"], 1)
            for r in range(PAIRS):
                dve.wait_ge(s["mr_ps"], r + 1)
                v.tensor_scalar(MRT[:, r].rearrange("p c n -> p (c n)"), bank(r), FMIN, None, ALU.max).then_inc(s["mrt_done"], 1)
            for r in range(PAIRS):
                dve.wait_ge(s["rt_ps"], r + 1)
                ins = v.tensor_copy(QT[:, r, :], bank(4 + r)[:, 0:128]).then_inc(s["qt_done"], 1)

            def kbd(b):
                if b >= 2:
                    dve.wait_ge(s["sc_ps"], b - 1)
                o = 128 + 64 * (b % 2)
                v.tensor_tensor(KBD[:, b % 2], bank(4 + b // 2)[:, o:o + 64].unsqueeze(1).to_broadcast([128, H, SLOT]),
                                cc("head").unsqueeze(2).to_broadcast([128, H, SLOT]), ALU.mult).then_inc(s["kbd_done"], 1)

            def softmax_in(r):
                dve.wait_ge(s["sc_ps"], 2 * r + 2)
                if r >= 2:
                    dve.wait_ge(s["at_ps"], r - 1)
                a = AE[:, r % 2, :, 0:CAP]
                for k in range(2):
                    ins = v.scalar_tensor_tensor(out=AE[:, r % 2, 8 * k:8 * k + 8, 0:CAP],
                                           in0=bank(2 * (r % 2) + k).rearrange("p (h n) -> p h n", h=8)[:, :, 0:CAP],
                                           scalar=SC0, in1=MS[:, r, 0:CAP].unsqueeze(1).to_broadcast([128, 8, CAP]),
                                           op0=ALU.mult, op1=ALU.add)
                ins.then_inc(s["smx_done"], 1)
                dve.wait_ge(s["smx_done"], r + 1)
                link(v.tensor_reduce(am[:, 0, r, :], a, AX.X, ALU.max))
                v.tensor_tensor(a, a, am[:, 0, r, :].unsqueeze(2).to_broadcast([128, H, CAP]), ALU.subtract
                                ).then_inc(s["ae_done"], 1)

            def softmax_sum(r):
                dve.wait_ge(s["exp_mod"], r + 1)
                link(v.tensor_reduce(am[:, 1, r, :], AE[:, r % 2, :, 0:CAP], AX.X, ALU.add))
                link(v.reciprocal(am[:, 2, r, :], am[:, 1, r, :]))

            kbd(0)
            kbd(1)
            for r in range(PAIRS):
                dve.wait_ge(s["ms_ps"], r + 1)
                v.tensor_copy(MS[:, r, :], bank(r)[:, 0:SLOT]).then_inc(s["ms_done"], 1)
            dve.wait_ge(s["ms_done"], PAIRS)
            kbd(2)
            kbd(3)
            softmax_in(0)
            kbd(4)
            kbd(5)
            softmax_in(1)
            kbd(6)
            kbd(7)
            softmax_sum(0)
            softmax_in(2)
            softmax_sum(1)
            softmax_in(3)
            softmax_sum(2)
            softmax_sum(3)
            for r in range(PAIRS):
                dve.wait_ge(s["op_ps"], r + 1)
                v.tensor_tensor(OO[:, r, :].rearrange("p (h n) -> p h n", h=H),
                                bank(r)[:, 0:D].rearrange("p (h n) -> p h n", h=H),
                                am[:, 2, r, :].unsqueeze(2).to_broadcast([128, H, HD0]), ALU.mult).then_inc(s["oo_done"], 1)
            for r in range(PAIRS):
                dve.wait_ge(s["wo_ps"], r + 1)
                v.tensor_tensor(X1S[:, r, :], XS[:, r, 0:D], bank(r)[:, 0:D], ALU.add).then_inc(s["x1s_done"], 1)
            dve.wait_ge(s["std_done"], 3)
            inv_sqrt(sm[:, 5, 0:PAIRS], RMS_EPS, 1.0 / D, sm[:, 6, 0:PAIRS], s["rstd_done"], PAIRS)
            dve.wait_ge(s["rstd_done"], 3)
            for r in range(PAIRS):
                v.scalar_tensor_tensor(out=H2[:, r, :], in0=X1S[:, r, :], scalar=sm[:, 2, r:r + 1], in1=rr("ln2"),
                                       op0=ALU.mult, op1=ALU.mult).then_inc(s["h2_done"], 1)
            for r in range(PAIRS):
                dve.wait_ge(s["w2_ps"], r + 1)
                link(v.tensor_tensor(PR[:, r, :], X1S[:, r, :], bank(r)[:, 256:384], ALU.add))
                v.tensor_scalar(PR[:, r, :], PR[:, r, :], XS[:, r, D + 8:D + 9], None, ALU.mult).then_inc(s["pr_done"], 1)
            for b in range(B):
                dve.wait_ge(s["scat_ps"], b + 1)
                dve.wait_ge(s["x1b_done"], b + 1)
                for c in range(C):
                    t = C * b + c
                    ins = v.scalar_tensor_tensor(out=XN[:, t, 0:D], in0=XN[:, t, 0:D], scalar=TS[:, c, 32 + b:33 + b],
                                                 in1=bank(4 + b % 4)[:, 128 * c:128 * c + 128], op0=ALU.mult, op1=ALU.add)
                ins.then_inc(s["ffn_done"], 1)

            def smax(n, p, h, slots=(0, 1)):
                for k in slots:
                    dve.wait_ge(s["s_full"], n * 2 + k + 1)
                    v.tensor_reduce(mx[:, p, 4 * h + 2 * k:4 * h + 2 * k + 2], PS[:, 2 * k:2 * k + 2, :], AX.X, ALU.max
                                    ).then_inc(s["s_free"], 1)

            def mt_copy(n, p):
                dve.wait_ge(s["mt_ps"], n + 1)
                v.tensor_scalar(mT[:, p, :], bank(7)[0:16, 0:128], -1.0, None, ALU.mult).then_inc(s["mt_sb"], 1)

            def normal(b, g):
                dve.wait_ge(s["ot_ps"], at(b, 4, g + 1))
                o = bank(7).rearrange("p (c h n) -> p c h n", c=C, h=HG)
                v.reciprocal(rd0, o[:, :, :, 8]).then_inc(s["rd_done"], 1)
                dve.wait_ge(s["rd_done"], at(b, 4, g + 1))
                v.tensor_tensor(OQ0[:, :, 32 * g:32 * g + 32].rearrange("p c (h n) -> p c h n", h=HG), o[:, :, :, 0:8],
                                rd0.unsqueeze(3).to_broadcast([128, C, HG, 8]), ALU.mult).then_inc(s["oq_done"], 1)

            def ot_copy(b):
                dve.wait_ge(s["otT_ps"], b + 1)
                v.tensor_copy(OT0, bank(7)).then_inc(s["otT_sb"], 1)

            def residual(b):
                dve.wait_ge(s["proj_ps"], b + 1)
                dst = X1[:, C * b:C * b + C, :] if isinstance(b, int) else X1[:, bass.ds(b * C, C), :]
                v.tensor_tensor(dst, dst, bank(7).rearrange("p (c n) -> p c n", c=C), ALU.add).then_inc(s["x1_l0"], 1)

            def steps0(b, first=False, last=False):
                for u in range(16):
                    g, kc = u // 4, u % 4
                    if u == 5 and not first:
                        ot_copy(b - 1)
                    if u == 6 and not first:
                        residual(b - 1)
                    if not (last and u >= 8):
                        u2 = (u + 8) % 16
                        nb = b if u < 8 else b + 1
                        smax(at(nb, 16, u2), (u2 // 4) % 2, u2 % 4, (0,))
                    if kc == 0 and not (last and g == 3):
                        mt_copy(at(b, 4, g + 1), (g + 1) % 2)
                    if not (last and u >= 8):
                        smax(at(nb, 16, u2), (u2 // 4) % 2, u2 % 4, (1,))
                    if kc == 2 and not (first and g == 0):
                        if g == 0:
                            normal(b - 1, 3)
                        else:
                            normal(b, g - 1)

            dve.wait_ge(s["mod_x1"], B)
            v.memset(bank(6), 0.0).then_inc(s["av_zero"], 1)
            for h in range(8):
                smax(h, h // 4, h % 4)
            mt_copy(0, 0)
            steps0(0, first=True)
            with dve.Fori(1, B - 1) as i:
                steps0(i)
            steps0(B - 1, last=True)
            normal(B - 1, 3)
            ot_copy(B - 1)
            residual(B - 1)

            dve.wait_ge(s["x1_l0"], B)
            for t in range(B * C):
                ins = v.bn_stats(st6[:, t, :], X1[:, t, :])
            link(ins)
            for t in range(B * C):
                ins = v.bn_aggr(mv[:, t, :], st6[:, t, :])
            ins.then_inc(s["stats_done"], 1)
            dve.wait_ge(s["stats_done"], 2)
            dve.wait_ge(s["std_done"], 4)
            inv_sqrt(mv[:, :, 1], LN_EPS, 1.0, sm[:, 0, :], s["rstd_done"], B * C)
            dve.wait_ge(s["rstd_done"], 4)

            def norm1(b):
                if b >= 2:
                    dve.wait_ge(s["xt2_ps"], b - 1)
                for c in range(C):
                    t = C * b + c
                    ins = v.tensor_scalar(xb1[b % 2][:, c, :], X1[:, t, :], mv[:, t, 0:1], sm[:, 2, t:t + 1], ALU.subtract,
                                          ALU.mult)
                ins.then_inc(s["xb_done"], 1)

            def add_lora(b):
                dve.wait_ge(s["lora_ps"], b + 1)
                xo = X1[:, C * b:C * b + C, :]
                v.tensor_tensor(xo, xo, bank(7).rearrange("p (c n) -> p c n", c=C), ALU.add).then_inc(s["x1_l1"], 1)

            def cps():
                return PS[:, 5:7, :].rearrange("p b (c n) -> p (b c) n", c=2)

            norm1(0)
            norm1(1)
            for b in range(B):
                p = b % 2
                if b + 2 < B:
                    norm1(b + 2)
                for a in range(2):
                    m = 4 * b + 2 * a
                    dve.wait_ge(s["p1_part1"], m + 1)
                    if m >= 2:
                        dve.wait_ge(s["p1_part3"], m - 1)
                    v.tensor_tensor(rem1[:, 0, 0:S], bank(2), pq1[:, p, 0, a, :], ALU.subtract).then_inc(s["p1_rem"], 1)
                    dve.wait_ge(s["p1_part1"], m + 2)
                    if m >= 2:
                        dve.wait_ge(s["p1_part3"], m)
                    v.tensor_tensor(rem1[:, 1, 0:ENC], bank(4)[:, 0:ENC], pk1[:, p, 0, a, 0:ENC], ALU.subtract)
                    v.tensor_tensor(rem1[:, 1, ENC:KEYS], bank(3), pk1[:, p, 0, a, ENC:KEYS], ALU.subtract
                                    ).then_inc(s["p1_rem"], 1)
                dve.wait_ge(s["cb_ps"], b + 1)
                link(v.tensor_tensor(LG[:, 2], cps()[:, :, D:D + E], rr("rb").unsqueeze(1).to_broadcast([128, C, E]), ALU.add))
                link(v.tensor_reduce(lmx[:, 0, :], LG[:, 2], AX.X, ALU.max))
                v.tensor_tensor(LG[:, 0], LG[:, 2], lmx[:, 0, :].unsqueeze(2).to_broadcast([128, C, E]), ALU.subtract
                                ).then_inc(s["lmax_done"], 1)
                xo = X1[:, C * b:C * b + C, :]
                dve.wait_ge(s["base_done"], b + 1)
                link(v.tensor_tensor(xo, xo, cps()[:, :, 0:D], ALU.add))
                dve.wait_ge(s["lexp"], b + 1)
                link(v.tensor_reduce(lmx[:, 1, :], LG[:, 1], AX.X, ALU.add))
                link(v.reciprocal(lmx[:, 2, :], lmx[:, 1, :]))
                link(v.tensor_tensor(GB, LG[:, 1], lmx[:, 2, :].unsqueeze(2).to_broadcast([128, C, E]), ALU.mult))
                for c in range(C):
                    ins = v.scalar_tensor_tensor(out=GM[:, p, c, :].rearrange("p (e r) -> p e r", e=E),
                                                 in0=GB[:, c, :].unsqueeze(2).to_broadcast([128, E, R]), scalar=2.0,
                                                 in1=cps()[:, c, D + E:D + E + R].unsqueeze(1).to_broadcast([128, E, R]),
                                                 op0=ALU.mult, op1=ALU.mult)
                ins.then_inc(s["gm_done"], 1)
                if b:
                    add_lora(b - 1)
            add_lora(B - 1)
            dve.wait_ge(s["x1_l1"], B)
            v.memset(bank(5), 0.0).then_inc(s["kpad"], 1)
            v.memset(V1[64:128, :, 4, :], 0.0).then_inc(s["v1_zero"], 1)

            def masked(b, g, h):
                dve.wait_ge(s["sq1d"], at(b, 64, 16 * g + 4 * h + 4))
                pv = P1[:, g % 2, h, :]
                v.scalar_tensor_tensor(out=pv, in0=pv, scalar=1.0, in1=cc("keep"), op0=ALU.add, op1=ALU.mult
                                       ).then_inc(s["mask1"], 1)

            def y_copy(b, g, a, p, free):
                dve.wait_ge(s["y_ps"], at(b, 8, 2 * g + a + 1))
                if free is not None:
                    dve.wait_ge(s["wout_ps"], free)
                v.tensor_copy(Y1[:, p, a, :], bank(3 + a)).then_inc(s["y_cp"], 1)

            def den_copy(b, g, p):
                dve.wait_ge(s["den_ps"], at(b, 4, g + 1))
                v.tensor_copy(dn1[:, p, :], bank(5)).then_inc(s["den_cp"], 1)

            def recip(b, g, p):
                dve.wait_ge(den_in, at(b, 64, 16 * g + 16))
                v.reciprocal(zR[:, p, :], dR[:, p, :]).then_inc(s["rec1"], 1)

            def add_out(b):
                dve.wait_ge(s["wout_ps"], at(b, 4, 4))
                dst = X1[:, C * b:C * b + C, :] if isinstance(b, int) else X1[:, bass.ds(b * C, C), :]
                v.tensor_tensor(dst, dst, bank(7).rearrange("p (c n) -> p c n", c=C), ALU.add).then_inc(s["out_add"], 1)

            def prev(b, g, k):
                return (b, g - k) if g >= k else (b - 1, g - k + G)

            def steps1(b, first=False, last=False):
                for g in range(G):
                    p = (g - 1) % 2
                    masked(b, g, 0)
                    if g == 2 and not first:
                        add_out(b - 1)
                    masked(b, g, 1)
                    if not (first and g < 2):
                        recip(*prev(b, g, 2), g % 2)
                    for a in range(2):
                        if not (first and g == 0):
                            y_copy(*prev(b, g, 1), a, p, None if first and g < 3 else at(b, 4, g - 2))
                        masked(b, g, 2 + a)
                    if not (first and g == 0):
                        den_copy(*prev(b, g, 1), p)

            steps1(0, first=True)
            with dve.Fori(1, B - 1) as i:
                steps1(i)
            steps1(B - 1, last=True)
            recip(B - 1, 2, 0)
            den_copy(B - 1, 3, 1)
            y_copy(B - 1, 3, 0, 1, 30)
            recip(B - 1, 3, 1)
            y_copy(B - 1, 3, 1, 1, 30)
            add_out(B - 1)

        @block.gpsimd
        def _(pool):
            g_ = nc.gpsimd
            for t in (KS, QS):
                g_.memset(t[:].rearrange("p g h n -> p (g h n)").bitcast(F32), 0.0).then_inc(s["ks_zero"], 1)
            pool.wait_ge(s["rows_in"], 16)
            for b in range(B):
                for k in range(2):
                    pool.wait_ge(s["part2"], 2 * b + k + 1)
                    g_.tensor_tensor(part0[b % 2][:, k, 2, :], rem0[:, k, :], part0[b % 2][:, k, 1, :], ALU.subtract
                                     ).then_inc(s["part3"], 1)
            pool.wait_ge(s["xn_done"], B)
            for b in range(B):
                xo = X1[:, C * b:C * b + C, :]
                g_.tensor_tensor(xo, xo, rr("projb").unsqueeze(1).to_broadcast([128, C, D]), ALU.add).then_inc(s["x1b_done"], 1)
            pool.wait_ge(s["idx_done"], 1)
            for r in range(PAIRS):
                g_.indirect_dma_start(out=MR[:, r, :], out_offset=None, in_=mask,
                                      in_offset=bass.IndirectOffsetOnAxis(ap=idx[:, r:r + 1], axis=0)).then_inc(mr_in, 16)
            for b in range(B):
                pool.wait_ge(s["ffn_done"], b + 1)
                xo = X1[:, C * b:C * b + C, :]
                g_.tensor_tensor(xo, xo, XN[:, C * b:C * b + C, 0:D], ALU.add).then_inc(s["mod_x1"], 1)

            one16 = cc("eps")[0:16, 3:4].to_broadcast([16, 128])

            def parts(n, p, first):
                pool.wait_ge(s["mt_sb"], n + 1)
                if not first:
                    pool.wait_ge(ext[p], (n * 24 - 24 * p) if not isinstance(n, int) else 48 * (n // 2))
                g_.tensor_tensor(mN[p][:, 0, :], mT[:, p, :], one16, ALU.mult).then_inc(s["chain_p"], 1)
                pool.wait_ge(s["chain_p"], n * 3 + 1)
                g_.tensor_tensor(mR, mT[:, p, :], mN[p][:, 0, :], ALU.subtract).then_inc(s["chain_p"], 1)
                pool.wait_ge(s["chain_p"], n * 3 + 2)
                g_.tensor_tensor(mN[p][:, 1, :], mR, one16, ALU.mult).then_inc(s["chain_p"], 1)
                pool.wait_ge(s["chain_p"], n * 3 + 3)
                g_.tensor_tensor(mN[p][:, 2, :], mR, mN[p][:, 1, :], ALU.subtract).then_inc(s["mn_done"], 1)
                pool.wait_ge(s["mn_done"], n + 1)

            for n in range(4):
                parts(n, n % 2, n < 2)
            with pool.Fori(1, B) as i:
                for g in range(G):
                    parts(at(i, 4, g), g % 2, False)

            pool.wait_ge(s["stats_done"], 2)
            for b in range(B):
                p = b % 2
                pool.wait_ge(s["xb_done"], b + 1)
                xo = X1[:, C * b:C * b + C, :]
                g_.tensor_tensor(xo, xo, rr("baseb").unsqueeze(1).to_broadcast([128, C, D]), ALU.add).then_inc(s["base_done"], 1)
                for a in range(2):
                    for k in range(2):
                        m = 4 * b + 2 * a + k
                        t, n = ((pq1, S), (pk1, KEYS))[k]
                        pool.wait_ge(s["part2"], 2 * B + m + 1)
                        g_.tensor_tensor(t[:, p, 2, a, :], rem1[:, k, 0:n], t[:, p, 1, a, :], ALU.subtract
                                         ).then_inc(s["p1_part3"], 1)

            def scale_y(n, p):
                pool.wait_ge(z_in, n * 64 + 64)
                for a in range(2):
                    pool.wait_ge(s["y_cp"], n * 2 + a + 1)
                    g_.tensor_tensor(Y1[:, p, a, :], Y1[:, p, a, :], Z1[:, p, a, :], ALU.mult).then_inc(s["yn1"], 1)

            with pool.Fori(0, B) as i:
                for g in range(G):
                    scale_y(at(i, 4, g), g % 2)


_OUT = ((B, S, D), "float32")


def kernel(**inputs):
    import concourse.bacc as _bacc
    from concourse import mybir as _mybir
    from concourse.bass_utils import run_bass_kernel_spmd as _run

    def a(name):
        return np.asarray(inputs[name])

    def wide(v):
        return np.broadcast_to(v.reshape(1, -1), (128, v.size))

    qkv = a("L0_attn_qkv_w")
    qkb = a("L0_attn_qkv_b")
    w0 = np.concatenate([qkv[:, 0:D], qkv[:, D:2 * D], qkv[:, 2 * D:], a("L0_ffn_router_w"), a("L0_attn_proj_w"),
                         a("L0_ffn_wq"), a("L0_ffn_wk"), a("L0_ffn_wv"), a("L0_ffn_wo"), a("L0_ffn_w1"),
                         a("L0_ffn_w2").reshape(F // 128, 128, D).transpose(1, 0, 2).reshape(128, F)], axis=1)
    w1 = np.concatenate([a("L1_attn_Wq").T, a("L1_attn_Wk").T, a("L1_attn_Wk_enc").T, a("L1_attn_Wv").T,
                         a("L1_attn_Wv_enc").T,
                         a("L1_attn_Wout").T.reshape(H // 2, 128, D).transpose(1, 0, 2).reshape(128, H * HD1),
                         a("L1_ffn_base_w").T, a("L1_ffn_router_w").T, a("L1_ffn_lora_A")], axis=1)
    rows = np.concatenate([wide(qkb[2 * D:]), wide(a("L0_attn_proj_b")), wide(a("L1_ffn_base_b")), wide(a("L0_ffn_ln1")),
                           wide(a("L0_ffn_ln2")), wide(a("L1_ffn_router_b")), wide(a("L0_ffn_router_b")),
                           qkb[0:2 * D].reshape(2, D).T], axis=1)
    arrays = {
        "x": a("L0_attn_x"), "consts": constants(), "rows": rows, "w0": w0, "w1": w1,
        "lora_b": a("L1_ffn_lora_B").reshape(E * R, D), "mask": a("L0_ffn_attention_mask").reshape(MB * S, S),
        "pos": a("L0_ffn_position_ids").reshape(MB * C, 128).T, "ones_rows": np.ones((3, G, HG, KPAD), _mybir.dt.np(BF16)),
    }
    arrays = {f"in_{k}": np.ascontiguousarray(v) for k, v in arrays.items()}
    nc = _bacc.Bacc("TRN2", target_bir_lowering=False, num_devices=1)
    args = [nc.dram_tensor(k, v.shape, _mybir.dt.from_np(v.dtype), kind="ExternalInput").ap() for k, v in arrays.items()]
    args.append(nc.dram_tensor("out_dram", _OUT[0], _mybir.dt.from_np(np.dtype(_OUT[1])), kind="ExternalOutput").ap())
    build(nc, *args)
    r = _run(nc, [arrays], core_ids=[0])
    return r.results[0]["out_dram"]
```

```python
import numpy as np

import concourse.bass as bass
from concourse import mybir
from contextlib import ExitStack

F32 = mybir.dt.float32
BF16 = mybir.dt.bfloat16
I32 = mybir.dt.int32
ALU = mybir.AluOpType
ACT = mybir.ActivationFunctionType
AX = mybir.AxisListType

B, S, D = 8, 512, 128
C = S // 128
H, HD0 = 16, 8
FD, HD1 = 16, 64
HG = 4
G = H // HG
TERMS = 6
ENC = 64
CAP = 63
SLOT = 64
RING = 4
PAIRS = B // 2
F = 512
MB = 4
E, R = 8, 8
NEG = -3.0e38
FMIN = -3.4028235e38
LN_EPS, RMS_EPS = 1e-5, 1e-6
SC0 = float(HD0) ** -0.5
XW = D + 10
KEYS = ENC + S
KPAD = 640
BLK_Q = [0, 64, 192, 320, 384]
BLK_N = [S - q for q in BLK_Q]
BLK_O = [sum(BLK_N[:j]) for j in range(5)]
PW = sum(BLK_N)


def columns(parts):
    at, out = 0, {}
    for name, n in parts:
        out[name] = (at, at + n)
        at += n
    return out, at


CONST, NCONST = columns([("ident", 128), ("iota", SLOT), ("head", H), ("keep", PW), ("token", B * C),
                         ("off", PAIRS), ("eps", 4)])
ROWS, NROWS = columns([("vb", D), ("projb", D), ("baseb", D), ("ln1", D), ("ln2", D), ("rb", E), ("mrb", 1),
                       ("qkb", 2)])
W0, NW0 = columns([("q", D), ("k", D), ("vr", D + 1), ("proj", D), ("mqkv", 3 * D), ("wo", D), ("w1", F),
                   ("w2", F)])
W1, NW1 = columns([("q", H * FD), ("k", H * FD), ("ke", H * FD), ("v", H * HD1), ("ve", H * HD1),
                   ("out", H * HD1), ("comb", D + E + R)])

AREA = {}
_at = 0
for _n, _w in [("ST", PAIRS * 512), ("MR", PAIRS * 512), ("MRT", PAIRS * 512), ("MS", PAIRS * SLOT),
               ("XS", PAIRS * XW), ("HN", PAIRS * D), ("HT", PAIRS * D), ("QKV", PAIRS * 3 * D),
               ("RQ", PAIRS * 2 * D), ("AB", 4 * D), ("KBD", 2 * H * SLOT),
               ("AE", 2 * H * SLOT), ("AT", 2 * 8 * D), ("VBD", B * D)]:
    AREA[_n] = (_at, _at + _w)
    _at += _w
NAREA = max(_at, 4 * PW + 6528 + G * 5 * 256)


def constants():
    c = np.zeros((128, NCONST), np.float32)
    p = np.arange(128)[:, None]

    def put(name, a):
        c[:, CONST[name][0]:CONST[name][1]] = a

    put("ident", np.eye(128))
    put("iota", np.arange(1, SLOT + 1)[None])
    put("head", p // HD0 == np.arange(H)[None])
    keep = np.zeros((128, PW), np.float32)
    for j in range(5):
        key = p + 128 * j - ENC
        q = BLK_Q[j] + np.arange(BLK_N[j])[None]
        keep[:, BLK_O[j]:BLK_O[j] + BLK_N[j]] = (key <= q) & (key < S)
    put("keep", keep)
    put("token", 128 * (np.arange(B * C) % C)[None] + p)
    put("off", S * np.minimum(2 * np.arange(PAIRS)[None] + p // SLOT, MB - 1))
    put("eps", np.array([LN_EPS, RMS_EPS, np.pi / 2, 1.0])[None])
    return c


def at(v, k, c):
    return v * k + c


def build(nc, x, consts, rows, w0, w1, lora_b, mask, pos, ones_rows, out):
    ctx = ExitStack()
    with ctx:
        def sb(name, shape, dt=F32):
            return ctx.enter_context(nc.sbuf_tensor(name, shape, dt))

        def sem(name):
            return ctx.enter_context(nc.semaphore(name))

        def dram(name, shape, dt=F32):
            return nc.dram_tensor(name, shape, dt, kind="Internal").ap()

        PS = ctx.enter_context(nc.psum_tensor("PS", [128, 8, 512], F32))
        X1 = sb("X1", [128, B * C, D])
        XN = sb("XN", [128, B * C, XW])
        cst = sb("cst", [128, NCONST])
        row = sb("row", [128, NROWS])
        w0s = sb("w0s", [128, NW0])
        w1s = sb("w1s", [128, NW1])
        lbs = sb("lbs", [E * R, D])
        QS = sb("QS", [128, G, HG, S], BF16)
        KS = sb("KS", [128, G, HG, KPAD], BF16)
        AR = sb("AR", [128, NAREA])
        V0 = sb("V0", [128, G, C, HG, 9])
        PB = sb("PB", [128, 6800])
        st6 = sb("st6", [128, B * C, 6])
        mv = sb("mv", [128, B * C, 2])
        sm = sb("sm", [128, 8, B * C])
        WT = sb("WT", [128, B * C])

        def cc(name, t=cst, d=CONST):
            return t[:, d[name][0]:d[name][1]]

        ident = cc("ident")

        def rr(name):
            return cc(name, row, ROWS)

        def ww0(name):
            return cc(name, w0s, W0)

        def ww1(name):
            return cc(name, w1s, W1)

        def ar(name):
            return AR[:, AREA[name][0]:AREA[name][1]]

        sqk0 = dram("sqk0", (B, 2, 3, HD0, H, S), BF16)
        sv0 = dram("sv0", (B, G, 128, C * HG * 9))
        sw = dram("sw", (B * C, 128))
        sq1 = dram("sq1", (B, 3, FD, H, S), BF16)
        sk1 = dram("sk1", (B, 3, FD, H, KEYS), BF16)
        sx1 = dram("sx1", (B, 128, S))
        sz = dram("sz", (2, HG, S))

        xT0 = [PB[:, 512 * p:512 * p + 512] for p in range(2)]
        part0 = [AR[:, 1536 * p:1536 * p + 1536].bitcast(BF16).rearrange("p (q t n) -> p q t n", q=2, t=3)
                 for p in range(RING)]
        rem0 = PB[:, 4096:5120].rearrange("p (q n) -> p q n", q=2)
        vb0 = [PB[:, 1024 + 576 * p:1600 + 576 * p].rearrange("p (g c h n) -> p g c h n", g=G, c=C, h=HG)
               for p in range(RING)]
        wrow = PB[0:32, 6272:6400]
        P0 = AR[:, 0:8192].rearrange("p (u h n) -> p u h n", u=4, h=HG)
        OS0 = PB[:, 0:512]
        OQ0 = PB[:, 512:1024].rearrange("p (c n) -> p c n", c=C)
        OT0 = PB[:, 1024:1536]
        mx = PB[:, 6736:6768].rearrange("p (s n) -> p s n", s=2)
        rd0 = PB[:, 1568:1584].rearrange("p (c h) -> p c h", c=C)
        mT = PB[0:16, 1600:1856].rearrange("p (s n) -> p s n", s=2)
        mR = PB[0:16, 1856:1984]
        mN = [PB[0:16, 2048 + 192 * p:2240 + 192 * p].bitcast(BF16).rearrange("p (t n) -> p t n", t=3)
              for p in range(2)]
        ST = ar("ST").rearrange("p (r c n) -> p r c n", r=PAIRS, c=C)
        MR = ar("MR").rearrange("p (r n) -> p r n", r=PAIRS)
        MRT = ar("MRT").rearrange("p (r c n) -> p r c n", r=PAIRS, c=C)
        MS = ar("MS").rearrange("p (r n) -> p r n", r=PAIRS)
        XS = ar("XS").rearrange("p (r n) -> p r n", r=PAIRS)
        HN = ar("HN").rearrange("p (r n) -> p r n", r=PAIRS)
        HT = ar("HT").rearrange("p (r n) -> p r n", r=PAIRS)
        QKV = ar("QKV").rearrange("p (r n) -> p r n", r=PAIRS)
        RQ = ar("RQ").rearrange("p (r n) -> p r n", r=PAIRS)
        AB = ar("AB").rearrange("p (a n) -> p a n", a=2)
        KBD = ar("KBD").rearrange("p (s h n) -> p s h n", s=2, h=H)
        AE = ar("AE").rearrange("p (s h n) -> p s h n", s=2, h=H)
        AT = ar("AT").rearrange("p (s k n) -> p s k n", s=2, k=8)
        VBD = ar("VBD").rearrange("p (b k n) -> p b k n", b=B, k=8)
        GT = ar("MR").rearrange("p (r f n) -> p r f n", r=PAIRS, f=4)
        SS = ar("MRT").rearrange("p (r c n) -> p r c n", r=PAIRS, c=C)
        OO, OOT, X1S, H2 = (ar("KBD")[:, 512 * i:512 * i + 512].rearrange("p (r n) -> p r n", r=PAIRS)
                            for i in range(4))
        H2T, PR = (ar("RQ")[:, 512 * i:512 * i + 512].rearrange("p (r n) -> p r n", r=PAIRS) for i in range(2))
        RS = ar("QKV")[0:96, 0:512]
        SEL = ar("QKV")[0:B, 512:1536].rearrange("p (a n) -> p a n", a=2)
        m8 = sb("m8", [B, 16])
        TS = PB[:, 5120:5504].rearrange("p (c n) -> p c n", c=C)
        idx = sb("idx", [128, PAIRS], I32)
        posi = sb("posi", [128, MB * C], I32)
        ang = PB[:, 6400:6720].rearrange("p (a n) -> p a n", a=5)
        am = PB[:, 5504:5504 + 3 * PAIRS * H].rearrange("p (a r h) -> p a r h", a=3, r=PAIRS)
        xT1 = [PB[:, 5696 + 512 * p:6208 + 512 * p] for p in range(2)]
        QP = 4 * PW
        pq1 = AR[:, QP:QP + 3072].bitcast(BF16).rearrange("p (s t a n) -> p s t a n", s=2, t=3, a=2)
        pk1 = AR[:, QP + 3072:QP + 6528].bitcast(BF16).rearrange("p (s t a n) -> p s t a n", s=2, t=3, a=2)
        XNF = XN[:].rearrange("p t n -> p (t n)")
        rem1 = XNF[:, 0:2 * KEYS].rearrange("p (a n) -> p a n", a=2)
        xb1 = [XNF[:, 2176 + 512 * p:2688 + 512 * p].rearrange("p (c n) -> p c n", c=C) for p in range(2)]
        LG = PB[:, 1024:1024 + 96].rearrange("p (a c e) -> p a c e", a=3, c=C)
        lmx = PB[:, 1136:1136 + 16].rearrange("p (a c) -> p a c", a=4)
        GB = PB[:, 1152:1168].bitcast(BF16).rearrange("p (c e) -> p c e", c=C)
        GM = PB[:, 1280:1280 + 512].rearrange("p (s c n) -> p s c n", s=2, c=C)
        GTT = PB[0:64, 1792:2816].rearrange("p (s n) -> p s n", s=2)
        P1 = AR[:, 0:8 * PW].rearrange("p (s h n) -> p s h n", s=2, h=HG)
        V1 = AR[:, QP + 6528:QP + 6528 + G * 1280].rearrange("p (g j n) -> p g j n", g=G, j=5)
        Y1 = PB[:, 0:2048].rearrange("p (s a n) -> p s a n", s=2, a=2)
        Z1 = PB[:, 2048:4096].rearrange("p (s a n) -> p s a n", s=2, a=2)
        dn1 = PB[:, 4096:5120].rearrange("p (s n) -> p s n", s=2)
        xTc = PB[:, 5120:5632]
        PSUMS = XNF[:, 0:2 * HG * S].rearrange("p (s h n) -> p s h n", s=2, h=HG)
        dR = PB[:, 5632:5664].rearrange("p (s n) -> p s n", s=2)
        zR = PB[:, 5664:5696].rearrange("p (s n) -> p s n", s=2)

        names = """consts_in rows_in keep_in w0_in w0b_in w1_in pos_in ones_in stats_done std_done rstd_done xn_done
            x1b_done xt_ps xt_sb qk_ps part1 rem_done part2 part3 v_ps v_sb wt_done wt_ps wt_row
            wrow_moved rs_done rs_ps ts_done onehot trig_r trig trig_done vzero g_ps xs_done
            idx_done mr_ps mrt_done ms_ps ms_done ssq_done hn_done ht_ps ht_sb mqkv_ps mqkv_sb
            rope_done rt_ps qt_done kbd_done sc_ps smx_done exp_mod ae_done at_ps at_sb vbd_done
            op_ps oo_done oot_ps oot_sb wo_ps x1s_done h2_done h2t_ps h2t_sb w1_ps
            gelu_done w2_ps pr_done ss_ps ss_sb scat_ps ffn_done mod_x1 chain_v chain_p ks_zero
            av_zero s_full s_free mt_ps mt_sb mn_done st_full exp_done av_done os_done ot_ps rd_done
            oq_done otT_ps otT_sb proj_ps x1_l0 xt2_ps xt2_sb qk1_ps p1_part1 p1_rem p1_part3
            cb_ps gm_done lexp gtr_ps gtr_sb lora_ps x1_l1 base_done lmax_done l1_zero sf1 sq1d
            mask1 sum_first sum_done v1_ps v1_cp y_ps y_cp den_ps den_cp rec1 yn1 wout_ps out_add xb_done""".split()
        s = {n: sem(n) for n in names}
        x_in = [sem(f"x_in{r}") for r in range(PAIRS)]
        wr0 = [sem(f"wr0_{p}") for p in range(RING)]
        wr1 = [sem(f"wr1_{p}") for p in range(2)]
        wrx = [sem(f"wrx_{p}") for p in range(2)]
        ld = [sem(f"ld{g}") for g in range(G)]
        ld1 = [sem(f"ld1_{g}") for g in range(G)]
        ext = [sem(f"ext{p}") for p in range(2)]
        mr_in = sem("mr_in")
        xt_in, den_in, z_out, z_in, outs = (sem(n) for n in ("xt_in", "den_in", "z_out", "z_in", "outs"))

        def bank(n):
            return PS[:, n, :]

        block = ctx.enter_context(nc.Block())

        def load_stacks(sp, g, d, q, k, n, done):
            heads = slice(HG * g, HG * g + HG)
            for first, part, times in ((0, 0, 3), (3, 1, 2), (5, 2, 1)):
                rows_ = slice(d * first, d * (first + times))
                src = q[part, :, heads].rearrange("d h n -> d (h n)")
                if times > 1:
                    src = src.unsqueeze(0).to_broadcast([times, d, HG * S])
                sp.dma_start(QS[rows_, g].rearrange("p h n -> p (h n)"), src).then_inc(done, 16)
                sp.dma_start(KS[rows_, g, :, 0:n], k[0:times, :, heads].rearrange("t d h n -> (t d) h n")).then_inc(done, 16)

        @block.sync
        def _(sp):
            CK, CW = CONST["keep"][0], W0["proj"][0]
            sp.dma_start(cst[:, 0:CK], consts[:, 0:CK]).then_inc(s["consts_in"], 16)
            sp.dma_start(cst[:, CONST["token"][0]:], consts[:, CONST["token"][0]:]).then_inc(s["consts_in"], 16)
            for b in range(B):
                sp.dma_start(X1[:, C * b:C * b + C, :], x[b].rearrange("(c p) d -> p c d", p=128)).then_inc(x_in[b // 2], 16)
                if b == 1:
                    sp.dma_start(row[:], rows).then_inc(s["rows_in"], 16)
                    sp.dma_start(w0s[:, 0:CW], w0[:, 0:CW]).then_inc(s["w0_in"], 16)
            sp.dma_start(posi[:], pos).then_inc(s["pos_in"], 16)
            sp.dma_start(w0s[:, CW:], w0[:, CW:]).then_inc(s["w0b_in"], 16)
            sp.dma_start(cst[:, CK:CONST["keep"][1]], consts[:, CK:CONST["keep"][1]]).then_inc(s["keep_in"], 16)
            sp.dma_start(w1s[:], w1).then_inc(s["w1_in"], 16)
            sp.dma_start(lbs[:], lora_b).then_inc(s["w1_in"], 16)
            sp.wait_ge(s["ks_zero"], 1)
            sp.dma_start(KS[96:99, :, :, :], ones_rows).then_inc(s["ones_in"], 16)
            for b in range(B):
                p = b % RING
                sp.wait_ge(s["part3"], 2 * b + 2)
                for k in range(2):
                    for t in range(3):
                        sp.dma_start(sqk0[b, k, t].rearrange("d h n -> h d n"), part0[p][:, k, t, :]).then_inc(wr0[p], 16)
                sp.wait_ge(s["v_sb"], b + 1)
                sp.dma_start(sv0[b].rearrange("g p n -> p g n"),
                             vb0[p].rearrange("p g c h n -> p g (c h n)")).then_inc(wr0[p], 16)
            for p in range(RING):
                sp.wait_ge(wr0[p], 16 * 7 * (B // RING))

            def stacks0(b, g, bp):
                if bp is not None:
                    sp.wait_ge(s["st_full"], at(bp, 64, 16 * (g + 1)))
                qk = sqk0[b] if isinstance(b, int) else sqk0[bass.ds(b, 1)].rearrange("o q t d h n -> (o q) t d h n")
                load_stacks(sp, g, HD0, qk[0], qk[1], S, ld[g])

            def values0(b, g, bp):
                if bp is not None:
                    sp.wait_ge(s["av_done"], at(bp, 16, 4 * (g + 1)))
                vv = sv0[b] if isinstance(b, int) else sv0[bass.ds(b, 1)].rearrange("o g p n -> (o g) p n")
                sp.dma_start(V0[:, g].rearrange("p c h n -> p (c h n)"), vv[g]).then_inc(ld[g], 16)

            def ext0(n2, p, g):
                sp.wait_ge(s["mn_done"], n2 * 2 - (1 - p))
                for t in range(3):
                    sp.dma_start(QS[96 + t:97 + t, g, :, :].rearrange("o h (c n) -> o (h c) n", c=C),
                                 mN[p][:, t, :]).then_inc(ext[p], 16)

            def steps0(b, first=False, last=False):
                for g in range(G):
                    old = None if first and g == 0 else (b, g - 1) if g else (b - 1, G - 1)
                    if old and not (last and g):
                        stacks0(old[0] + 1, old[1], old[0])
                    if not (last and g == 3):
                        ext0(at(b, 2, (g + 1) // 2 + 1), (g + 1) % 2, (g + 1) % G)
                    if old and not (last and g):
                        values0(old[0] + 1, old[1], old[0])

            sp.wait_ge(s["ks_zero"], 2)
            for g in range(G):
                stacks0(0, g, None)
                values0(0, g, None)
            ext0(1, 0, 0)
            steps0(0, first=True)
            with sp.Fori(1, B - 1) as i:
                steps0(i)
            steps0(B - 1, last=True)

            def load1(b, g, bp):
                if bp is not None:
                    sp.wait_ge(s["sf1"], at(bp, 64, 16 * (g + 1)))
                q, k = (t[b] if isinstance(b, int) else t[bass.ds(b, 1)].rearrange("o t d h n -> (o t) d h n")
                        for t in (sq1, sk1))
                load_stacks(sp, g, FD, q, k, KEYS, ld1[g])

            sp.wait_ge(s["x1_l0"], B)
            for b in range(B):
                p = b % 2
                sp.wait_ge(s["xt2_sb"], b + 1)
                if b >= 2:
                    sp.wait_ge(wrx[p], 16 * (b // 2))
                sp.dma_start(sx1[b], xT1[p]).then_inc(wrx[p], 16)
                sp.wait_ge(s["p1_part3"], 4 * b + 4)
                if b >= 2:
                    sp.wait_ge(wr1[p], 16 * 12 * (b // 2))
                for dst, src in ((sq1, pq1), (sk1, pk1)):
                    for a in range(2):
                        for t in range(3):
                            sp.dma_start(dst[b, t, :, 8 * a:8 * a + 8].rearrange("d h n -> h d n"), src[:, p, t, a, :]
                                         ).then_inc(wr1[p], 16)
                if b == 2:
                    sp.dma_start(xTc, sx1[0]).then_inc(xt_in, 16)
                if b in (3, 5):
                    load1(0, (b - 3) // 2, None)
            for p in range(2):
                sp.wait_ge(wrx[p], 16 * (B // 2))
                sp.wait_ge(wr1[p], 16 * 12 * (B // 2))

            def den_chain(n, p):
                sp.wait_ge(s["den_cp"], n + 1)
                sp.dma_start(dR[:, p, :], dn1[0:128:32, p, :]).then_inc(den_in, 16)
                sp.wait_ge(s["rec1"], n + 1)
                if not isinstance(n, int) or n >= 2:
                    sp.wait_ge(s["yn1"], n * 2 - 2)
                sp.dma_start(sz[p].rearrange("h (a n) -> (h a) n", n=16), zR[:, p, :]).then_inc(z_out, 16)
                sp.wait_ge(z_out, n * 16 + 16)
                for a in range(2):
                    for k in range(2):
                        sp.dma_start(Z1[64 * k:64 * k + 64, p, a, :],
                                     sz[p, 2 * a + k:2 * a + k + 1, :].to_broadcast([64, S])).then_inc(z_in, 16)

            def store(b, n):
                sp.wait_ge(s["out_add"], n)
                dst = out[b] if isinstance(b, int) else out[bass.ds(b, 1)].rearrange("o t d -> (o t) d")
                src = X1[:, C * b:C * b + C, :] if isinstance(b, int) else X1[:, bass.ds(b * C, C), :]
                sp.dma_start(dst.rearrange("(c p) d -> p c d", p=128), src).then_inc(outs, 16)

            def steps1(b, first=False, last=False):
                for g in range(G):
                    if not (first and g == 0):
                        den_chain(at(b, 4, g - 1), (g - 1) % 2)
                    if not last:
                        load1(b + 1, g, b)
                    if g == 2 and not first:
                        store(b - 1, b)

            for g in range(2, G):
                load1(0, g, None)
            steps1(0, first=True)
            with sp.Fori(1, B - 1) as i:
                steps1(i)
            steps1(B - 1, last=True)
            den_chain(B * G - 1, 1)
            store(B - 1, B)
            sp.wait_ge(outs, 16 * B)

        @block.tensor
        def _(pe):
            mm = nc.tensor.matmul

            def tr(o, i, k):
                return nc.tensor.transpose(o, i, ident[0:k, 0:k])

            pe.wait_ge(s["consts_in"], 32)
            pe.wait_ge(s["w0_in"], 16)

            def prep0_a(b):
                pe.wait_ge(s["xn_done"], b + 1)
                if b >= 2:
                    pe.wait_ge(s["xt_sb"], b - 1)
                for c in range(C):
                    last = tr(bank(b % 2)[:, 128 * c:128 * c + 128], XN[:, C * b + c, 0:D], 128)
                last.then_inc(s["xt_ps"], 1)

            def prep0_b(b):
                p = b % 2
                pe.wait_ge(s["xt_sb"], b + 1)
                if b >= 2:
                    pe.wait_ge(s["rem_done"], 2 * b - 2)
                mm(bank(2 + 2 * p), ww0("q"), xT0[p], start=True, stop=True).then_inc(s["qk_ps"], 1)
                mm(bank(3 + 2 * p), ww0("k"), xT0[p], start=True, stop=True).then_inc(s["qk_ps"], 1)
                if b >= 1:
                    pe.wait_ge(s["v_sb"], b)
                    pe.wait_ge(s["wt_done"], b)
                for c in range(C):
                    o = 256 * (c % 2)
                    last = mm(PS[:, 6 + c // 2, o:o + D + 1], xT0[p][:, 128 * c:128 * c + 128], ww0("vr"),
                              start=True, stop=True)
                last.then_inc(s["v_ps"], 1)

            prep0_a(0)
            for b in range(B):
                if b + 1 < B:
                    prep0_a(b + 1)
                prep0_b(b)

            pe.wait_ge(s["wt_done"], B)
            tr(bank(0)[0:32, 0:128], WT[:], 128).then_inc(s["wt_ps"], 1)
            pe.wait_ge(s["rs_done"], 1)
            pe.wait_ge(s["rem_done"], 2 * B)
            for c in range(C):
                last = tr(bank(1)[:, 96 * c:96 * c + 96], RS[:, 128 * c:128 * c + 128], 96)
            last.then_inc(s["rs_ps"], 1)

            def halves(r):
                return [(2 * r + k, slice(64 * k, 64 * k + 64)) for k in range(2)]

            def s_pass(n, g, h, halves_=(0, 1)):
                for k in halves_:
                    if not isinstance(n, int) or 2 * n + k > 1:
                        pe.wait_ge(s["s_free"], n * 2 + k - 1)
                    for j in range(2):
                        q = 2 * k + j
                        last = mm(PS[:, 2 * k + j, :], QS[0:96, g, h, 128 * q:128 * q + 128], KS[0:96, g, h, 0:S],
                                  start=True, stop=True)
                    last.then_inc(s["s_full"], 1)

            def early_scores(first, n):
                for h in range(first, first + n):
                    if h % 4 == 0:
                        pe.wait_ge(ld[h // 4], 112)
                    s_pass(h, h // 4, h % 4)

            pe.wait_ge(s["w0b_in"], 16)
            pe.wait_ge(s["trig_done"], 1)
            pe.wait_ge(s["v_sb"], B)
            for r in range(PAIRS):
                pe.wait_ge(s["onehot"], r + 1)
                if r == 0:
                    pe.wait_ge(s["wt_row"], 1)
                if r == 1:
                    pe.wait_ge(s["ts_done"], 1)
                for c in range(C):
                    for b, hs in halves(r):
                        last = mm(bank(r)[hs, 0:XW], ST[:, r, c, hs], XN[:, C * b + c, :], start=(c == 0),
                                  stop=(c == C - 1))
                last.then_inc(s["g_ps"], 1)
            for r in range(PAIRS):
                pe.wait_ge(s["hn_done"], r + 1)
                tr(bank(4 + r)[:, 0:128], HN[:, r, :], 128).then_inc(s["ht_ps"], 1)
            for r in range(PAIRS):
                pe.wait_ge(s["ht_sb"], r + 1)
                mm(bank(r)[:, 0:3 * D], HT[:, r, :], ww0("mqkv"), start=True, stop=True).then_inc(s["mqkv_ps"], 1)
            for r in range(PAIRS):
                pe.wait_ge(s["rope_done"], r + 1)
                tr(bank(4 + r)[:, 0:128], RQ[:, r, 0:D], 128)
                tr(bank(4 + r)[:, 128:256], RQ[:, r, D:2 * D], 128).then_inc(s["rt_ps"], 1)
            for r in range(PAIRS):
                pe.wait_ge(mr_in, 16 * PAIRS)
                for c in range(C):
                    last = tr(bank(r)[:, 128 * c:128 * c + 128], MR[:, r, 128 * c:128 * c + 128], 128)
                last.then_inc(s["mr_ps"], 1)
            for r in range(PAIRS):
                pe.wait_ge(s["mrt_done"], r + 1)
                if r == 0:
                    pe.wait_ge(s["qt_done"], PAIRS)
                for b, hs in halves(r):
                    for c in range(C):
                        last = mm(bank(r)[hs, 0:SLOT], MRT[:, r, c, hs], ST[:, r, c, hs],
                                  start=(c == 0), stop=(c == C - 1))
                last.then_inc(s["ms_ps"], 1)

            def scores(r):
                pe.wait_ge(s["ms_done"], PAIRS)
                if r == 2:
                    pe.wait_ge(s["smx_done"], 1)
                if r == 3:
                    pe.wait_ge(s["smx_done"], 2)
                for b, hs in halves(r):
                    pe.wait_ge(s["kbd_done"], b + 1)
                    for k in range(2):
                        last = mm(bank(2 * (r % 2) + k)[hs, :], RQ[:, r, hs],
                                  KBD[:, b % 2, 8 * k:8 * k + 8, :].rearrange("p h n -> p (h n)"), start=True, stop=True)
                    last.then_inc(s["sc_ps"], 1)

            def att_t(r):
                pe.wait_ge(s["exp_mod"], r + 1)
                if r < 2:
                    pe.wait_ge(s["qt_done"], 2 * r + 2)
                else:
                    pe.wait_ge(s["at_sb"], r - 1)
                for k in range(8):
                    o = 4 + 2 * (r % 2) + k // 4
                    last = tr(bank(o)[:, 128 * (k % 4):128 * (k % 4) + 128],
                              AE[:, r % 2, 2 * k:2 * k + 2, :].rearrange("p h n -> p (h n)"), 128)
                last.then_inc(s["at_ps"], 1)

            def att_v(r):
                pe.wait_ge(s["at_sb"], r + 1)
                pe.wait_ge(s["vbd_done"], 2 * r + 2)
                for k in range(8):
                    for b, hs in halves(r):
                        last = mm(bank(r)[hs, 16 * k:16 * k + 16], AT[:, r % 2, k, hs], VBD[:, b, k, :],
                                  start=(k == 0), stop=(k == 7), skip_group_check=True)
                last.then_inc(s["op_ps"], 1)

            scores(0)
            scores(1)
            att_t(0)
            scores(2)
            att_t(1)
            scores(3)
            pe.wait_ge(s["smx_done"], PAIRS)
            att_v(0)
            att_t(2)
            att_v(1)
            att_t(3)
            att_v(2)
            att_v(3)
            for r in range(PAIRS):
                pe.wait_ge(s["oo_done"], r + 1)
                tr(bank(4 + r)[:, 0:128], OO[:, r, :], 128).then_inc(s["oot_ps"], 1)
            pe.wait_ge(s["ks_zero"], 2)
            early_scores(0, 1)
            for r in range(PAIRS):
                pe.wait_ge(s["oot_sb"], r + 1)
                mm(bank(4 + r)[:, 128:256], OOT[:, r, :], ww0("wo"), start=True, stop=True).then_inc(s["wo_ps"], 1)
            early_scores(1, 1)
            for r in range(PAIRS):
                pe.wait_ge(s["x1s_done"], r + 1)
                for c in range(C):
                    last = tr(bank(4 + r)[:, 128 * c:128 * c + 128], ST[:, r, c, :], 128)
                last.then_inc(s["ss_ps"], 1)
            for r in range(PAIRS):
                pe.wait_ge(s["ss_sb"], r + 1)
                pe.wait_ge(s["h2_done"], r + 1)
                tr(bank(4 + r)[:, 0:128], H2[:, r, :], 128).then_inc(s["h2t_ps"], 1)
            early_scores(2, 1)
            for r in range(PAIRS):
                pe.wait_ge(s["h2t_sb"], r + 1)
                for f in range(4):
                    last = mm(bank(4 + r)[:, 128 * f:128 * f + 128], ww0("w1")[:, 128 * f:128 * f + 128], H2T[:, r, :],
                              start=True, stop=True)
                last.then_inc(s["w1_ps"], 1)
                if r % 2:
                    early_scores(3 + r // 2, 1)
            for r in range(PAIRS):
                pe.wait_ge(s["gelu_done"], r + 1)
                for f in range(4):
                    last = mm(bank(4 + r)[:, 256:384], GT[:, r, f, :], ww0("w2")[:, 128 * f:128 * f + 128], start=(f == 0),
                              stop=(f == 3))
                last.then_inc(s["w2_ps"], 1)
                if r % 2:
                    early_scores(5 + r // 2, 1)
            pe.wait_ge(s["s_free"], 14)
            tr(bank(3)[0:16, 0:128], mx[:, 0, :], 128).then_inc(s["mt_ps"], 1)
            for b in range(B):
                r, hs = b // 2, slice(64 * (b % 2), 64 * (b % 2) + 64)
                pe.wait_ge(s["pr_done"], PAIRS)
                if b == 4:
                    pe.wait_ge(s["mt_sb"], 1)
                    early_scores(7, 1)
                if b >= 4:
                    pe.wait_ge(s["ffn_done"], b - 3)
                for c in range(C):
                    last = mm(bank(4 + b % 4)[:, 128 * c:128 * c + 128], SS[hs, r, c, :], PR[hs, r, :], start=True,
                              stop=True)
                last.then_inc(s["scat_ps"], 1)

            def max_t(n, p):
                pe.wait_ge(s["s_free"], n * 8 + 8)
                tr(bank(7)[0:16, 0:128], mx[:, p, :], 128).then_inc(s["mt_ps"], 1)

            def st_pass(b, g, kc, heads):
                if kc == 0 and heads[0] == 0:
                    pe.wait_ge(ext[g % 2], at(b, 96, 48 * (g // 2 + 1)))
                for h in heads:
                    k = 16 * g + 4 * kc + h
                    if not isinstance(b, int) or b * 64 + k >= 2:
                        pe.wait_ge(s["exp_done"], at(b, 64, k - 1))
                    mm(bank(4 + k % 2), KS[0:99, g, h, 128 * kc:128 * kc + 128], QS[0:99, g, h, :], start=True,
                       stop=True).then_inc(s["st_full"], 1)

            def av(b, u, half, first=False):
                g, kc = u // 4, u % 4
                if half == 0:
                    if first:
                        pe.wait_ge(s["av_zero"], 1)
                    pe.wait_ge(s["exp_done"], at(b, 64, 4 * u + 4))
                    if kc == 0 and not first:
                        pe.wait_ge(s["os_done"], at(b, 4, g))
                q = slice(256 * half, 256 * half + 256)
                for h in range(HG):
                    last = mm(PS[32 * h:32 * h + 9, 6, q], V0[:, g, kc, h, :], P0[:, u % 4, h, q],
                              start=(kc == 0 and half == 0), stop=(kc == C - 1), skip_group_check=True)
                if half == 1:
                    last.then_inc(s["av_done"], 1)

            def o_t(b, g):
                pe.wait_ge(s["os_done"], at(b, 4, g + 1))
                for c in range(C):
                    last = tr(bank(7)[:, 128 * c:128 * c + 128], OS0[:, 128 * c:128 * c + 128], 128)
                last.then_inc(s["ot_ps"], 1)

            def oq_t(b):
                pe.wait_ge(s["oq_done"], at(b, 4, 4))
                for c in range(C):
                    last = tr(bank(7)[:, 128 * c:128 * c + 128], OQ0[:, c, :], 128)
                last.then_inc(s["otT_ps"], 1)

            def proj(b):
                pe.wait_ge(s["otT_sb"], b + 1)
                for c in range(C):
                    last = mm(bank(7)[:, 128 * c:128 * c + 128], OT0[:, 128 * c:128 * c + 128], ww0("proj"),
                              start=True, stop=True)
                last.then_inc(s["proj_ps"], 1)

            def steps0(b, first=False, last=False):
                for u in range(16):
                    g, kc = u // 4, u % 4
                    if not (last and u >= 8):
                        u2 = (u + 8) % 16
                        nb = b if u < 8 else b + 1
                        if u2 % 4 == 0:
                            pe.wait_ge(ld[u2 // 4], at(nb, 112, 112))
                    st_pass(b, g, kc, (0, 1))
                    if not (last and u >= 8):
                        s_pass(at(nb, 16, u2), u2 // 4, u2 % 4, (0,))
                    before = (b, u - 2, first and u == 2) if u >= 2 else (b - 1, u + 14, False)
                    if u >= 2 or not first:
                        av(before[0], before[1], 0, before[2])
                    if kc == 0 and not (last and g == 3):
                        if not first or g > 1:
                            pe.wait_ge(s["oq_done"], at(b, 4, g - 1))
                        if first and g == 1:
                            pe.wait_ge(s["mt_sb"], 2)
                        max_t(at(b, 4, g + 1), (g + 1) % 2)
                    st_pass(b, g, kc, (2, 3))
                    if not (last and u >= 8):
                        s_pass(at(nb, 16, u2), u2 // 4, u2 % 4, (1,))
                    if u >= 2 or not first:
                        av(before[0], before[1], 1)
                    if kc == 2 and not (first and g == 0):
                        pe.wait_ge(s["mt_sb"], at(b, 4, g + 2) if not (last and g == 3) else 32)
                        if g == 1 and not first:
                            pe.wait_ge(s["x1_l0"], b)
                        if last and g == 3:
                            pe.wait_ge(s["oq_done"], 4 * B - 2)
                        if g == 0:
                            o_t(b - 1, 3)
                        else:
                            o_t(b, g - 1)
                    if u == 4 and not first:
                        pe.wait_ge(s["mt_sb"], at(b, 4, 3))
                        oq_t(b - 1)
                    if u == 5 and not first:
                        proj(b - 1)

            pe.wait_ge(s["ones_in"], 16)
            pe.wait_ge(s["ffn_done"], B)
            steps0(0, first=True)
            with pe.Fori(1, B - 1) as i:
                steps0(i)
            def prep1_a(b):
                pe.wait_ge(s["xb_done"], b + 1)
                if b:
                    pe.wait_ge(s["xt2_sb"], b)
                for c in range(C):
                    last = tr(bank(0)[:, 128 * c:128 * c + 128], xb1[b % 2][:, c, :], 128)
                last.then_inc(s["xt2_ps"], 1)

            steps0(B - 1, last=True)
            pe.wait_ge(s["s_free"], 2 * B * H)
            prep1_a(0)
            for u in (14, 15):
                for half in range(2):
                    av(B - 1, u, half)
            pe.wait_ge(s["oq_done"], 4 * B - 1)
            o_t(B - 1, 3)
            oq_t(B - 1)
            proj(B - 1)

            pe.wait_ge(s["w1_in"], 32)

            def gates_t(b):
                pe.wait_ge(s["gm_done"], b + 1)
                if b:
                    pe.wait_ge(s["x1_l1"], b)
                for c in range(C):
                    last = tr(bank(7)[0:64, 128 * c:128 * c + 128], GM[:, b % 2, c, :], 128)
                last.then_inc(s["gtr_ps"], 1)

            def prep1_b(b):
                p = b % 2
                pe.wait_ge(s["xt2_sb"], b + 1)
                for a in range(2):
                    f = slice(128 * a, 128 * a + 128)
                    for k, name in enumerate(("q", "k")):
                        m = 4 * b + 2 * a + k
                        if m >= 3:
                            pe.wait_ge(s["p1_rem"], m - 2)
                        if k and a == 0:
                            if b:
                                pe.wait_ge(s["p1_rem"], 4 * b)
                            for a2 in range(2):
                                mm(bank(4)[:, 128 * a2:128 * a2 + 128], ww1("ke")[:, 128 * a2:128 * a2 + 128],
                                   xT1[p][:, 0:128], start=True, stop=True)
                        mm(bank(1 + m % 3), ww1(name)[:, f], xT1[p], start=True, stop=True).then_inc(s["qk1_ps"], 1)
                    if a == 0 and b:
                        gates_t(b - 1)
                if b:
                    pe.wait_ge(s["gm_done"], b)
                for c in range(C):
                    o = 256 * (c % 2)
                    last = mm(PS[:, 5 + c // 2, o:o + D + E + R], xT1[p][:, 128 * c:128 * c + 128], ww1("comb"),
                              start=True, stop=True)
                last.then_inc(s["cb_ps"], 1)

            def prep1_c(b):
                p = b % 2
                pe.wait_ge(s["gtr_sb"], b + 1)
                for c in range(C):
                    last = mm(bank(7)[:, 128 * c:128 * c + 128], GTT[:, p, 128 * c:128 * c + 128], lbs[:], start=True,
                              stop=True)
                last.then_inc(s["lora_ps"], 1)

            for b in range(B):
                if b + 1 < B:
                    prep1_a(b + 1)
                prep1_b(b)
                if b:
                    prep1_c(b - 1)
            gates_t(B - 1)
            prep1_c(B - 1)

            ones32 = cc("eps")[:, 3:4]

            def st1(b, g, h, half):
                if h == 0 and half == 0:
                    pe.wait_ge(ld1[g], at(b, 96, 96))
                for k, blocks in list(enumerate(((0,), (1,), (2, 3), (4,))))[2 * half:2 * half + 2]:
                    n = 16 * g + 4 * h + k
                    m = 4 * h + k
                    if not isinstance(b, int) or 64 * b + n >= 3:
                        pe.wait_ge(s["sq1d"], at(b, 64, n - 2 if m else n))
                    o = 0
                    for j in blocks:
                        last = mm(bank(m % 3)[:, o:o + BLK_N[j]], KS[0:96, g, h, 128 * j:128 * j + 128],
                                  QS[0:96, g, h, BLK_Q[j]:S], start=True, stop=True)
                        o += BLK_N[j]
                    last.then_inc(s["sf1"], 1)

            def av1(b, g, a, blocks):
                if a == 0 and blocks[0] == 0:
                    pe.wait_ge(s["mask1"], at(b, 16, 4 * g + 4))
                    pe.wait_ge(s["v1_cp"], at(b, 12, 3 * g + 3))
                if blocks[0] == 0 and not (isinstance(b, int) and b == 0 and g == 0):
                    pe.wait_ge(s["y_cp"], at(b, 8, 2 * g + a - 1))
                for j in blocks:
                    for k in range(2):
                        h = 2 * a + k
                        last = mm(PS[64 * k:64 * k + 64, 3 + a, BLK_Q[j]:S], V1[:, g, j, 64 * h:64 * h + 64],
                                  P1[:, g % 2, h, BLK_O[j]:BLK_O[j] + BLK_N[j]], start=(j == 0), stop=(j == 4))
                if blocks[-1] == 4:
                    last.then_inc(s["y_ps"], 1)

            def den1(b, g):
                pe.wait_ge(s["sum_done"], at(b, 24, 6 * g + 6))
                if not (isinstance(b, int) and b == 0 and g == 0):
                    pe.wait_ge(s["den_cp"], at(b, 4, g))
                q = BLK_Q[1]
                for h in range(HG):
                    mm(PS[32 * h:32 * h + 1, 5, 0:q], ones32, P1[:, g % 2, h, 0:q], start=True, stop=True)
                for h in range(HG):
                    last = mm(PS[32 * h:32 * h + 1, 5, q:S], ones32, PSUMS[:, g % 2, h, q:S], start=False, stop=True,
                              skip_group_check=True)
                last.then_inc(s["den_ps"], 1)

            def v1(b, g, fills):
                if g == 0 and fills[0] == 0:
                    pe.wait_ge(xt_in, at(b, 16, 16))
                f = slice(256 * g, 256 * g + 256)
                for k in fills:
                    if not (isinstance(b, int) and b == 0 and g == 0 and k == 0):
                        pe.wait_ge(s["v1_cp"], at(b, 12, 3 * g + k))
                    if k == 0:
                        mm(PS[0:64, 6, 0:256], xTc[:, 0:64], ww1("ve")[:, f], start=True, stop=True)
                        mm(PS[64:128, 6, 0:256], xTc[:, 0:64], ww1("v")[:, f], start=True, stop=True)
                        last = mm(PS[:, 6, 256:512], xTc[:, 64:192], ww1("v")[:, f], start=True, stop=True)
                    elif k == 1:
                        mm(PS[:, 6, 0:256], xTc[:, 192:320], ww1("v")[:, f], start=True, stop=True)
                        last = mm(PS[:, 6, 256:512], xTc[:, 320:448], ww1("v")[:, f], start=True, stop=True)
                    else:
                        last = mm(PS[0:64, 6, 0:256], xTc[:, 448:512], ww1("v")[:, f], start=True, stop=True)
                    last.then_inc(s["v1_ps"], 1)

            def wout(b, g, a):
                pe.wait_ge(s["yn1"], at(b, 8, 2 * g + a + 1))
                if a == 0 and g == 0 and not (isinstance(b, int) and b == 0):
                    pe.wait_ge(s["out_add"], b)
                for c in range(C):
                    k = 2 * g + a
                    last = mm(bank(7)[:, 128 * c:128 * c + 128], Y1[:, g % 2, a, 128 * c:128 * c + 128],
                              ww1("out")[:, 128 * k:128 * k + 128], start=(k == 0 and c == 0), stop=(k == 7),
                              skip_group_check=True)
                if a == 1:
                    last.then_inc(s["wout_ps"], 1)

            def prev(b, g, k):
                return (b, g - k) if g >= k else (b - 1, g - k + G)

            def steps1(b, first=False, last=False):
                for g in range(G):
                    before = not (first and g == 0)
                    p1 = prev(b, g, 1) if before else None
                    vn = (b if g < 3 else b + 1, (g + 1) % G) if not (last and g == 3) else None
                    out_of = prev(b, g, 3) if not (first and g < 3) else None
                    for a in range(2):
                        st1(b, g, 0, a)
                        if out_of:
                            wout(*out_of, a)
                    for a in range(2):
                        st1(b, g, 1 + a, 0)
                        if a and vn:
                            v1(*vn, (0,))
                        if before:
                            av1(*p1, a, (0, 1))
                        st1(b, g, 1 + a, 1)
                        if before:
                            av1(*p1, a, (2, 3, 4))
                    st1(b, g, 3, 0)
                    if vn:
                        v1(*vn, (1,))
                    st1(b, g, 3, 1)
                    if before:
                        den1(*p1)
                    if vn:
                        v1(*vn, (2,))

            v1(0, 0, (0, 1, 2))
            pe.wait_ge(s["p1_rem"], 4 * B)
            pe.wait_ge(s["l1_zero"], 2)
            pe.wait_ge(s["x1_l1"], B)
            steps1(0, first=True)
            with pe.Fori(1, B - 1) as i:
                steps1(i)
            steps1(B - 1, last=True)
            every = (0, 1, 2, 3, 4)
            for a in range(2):
                wout(B - 1, 1, a)
            av1(B - 1, 3, 0, every)
            den1(B - 1, 3)
            av1(B - 1, 3, 1, every)
            for g in (2, 3):
                for a in range(2):
                    wout(B - 1, g, a)

        @block.scalar
        def _(act):
            A = nc.scalar.activation
            act.wait_ge(s["consts_in"], 32)
            for k, cols in enumerate((slice(0, 2 * C), slice(2 * C, B * C))):
                act.wait_ge(s["stats_done"], k + 1)
                A(sm[:, 0, cols], mv[:, cols, 1], ACT.Sqrt, bias=cc("eps")[:, 0:1]).then_inc(s["std_done"], 1)
            act.wait_ge(s["rows_in"], 16)

            def xt0_copy(b):
                act.wait_ge(s["xt_ps"], b + 1)
                if b >= 2:
                    act.wait_ge(s["v_ps"], b - 1)
                A(xT0[b % 2], bank(b % 2), ACT.Copy).then_inc(s["xt_sb"], 1)

            xt0_copy(0)
            for b in range(B):
                p = b % RING
                if b >= RING:
                    act.wait_ge(wr0[p], 16 * 7 * (b // RING))
                for k in range(2):
                    act.wait_ge(s["qk_ps"], 2 * b + k + 1)
                    A(part0[p][:, k, 0, :], bank(2 + 2 * (b % 2) + k), ACT.Identity, bias=rr("qkb")[:, k:k + 1]).then_inc(s["part1"], 1)
                if b + 1 < B:
                    xt0_copy(b + 1)
                for k in range(2):
                    act.wait_ge(s["rem_done"], 2 * b + k + 1)
                    A(part0[p][:, k, 1, :], rem0[:, k, :], ACT.Copy).then_inc(s["part2"], 1)
            act.wait_ge(s["wt_row"], 1)
            act.dma_start(sw, wrow).then_inc(s["wrow_moved"], 16)
            act.wait_ge(s["wrow_moved"], 16)
            act.dma_start(SEL[:, 0, :], sw.rearrange("(b c) n -> b (c n)", b=B)).then_inc(s["wrow_moved"], 16)
            act.wait_ge(s["trig_r"], 1)
            A(ang[:, 2, :], ang[:, 0, :], ACT.Sin)
            A(ang[:, 3, :], ang[:, 1, :], ACT.Sin).then_inc(s["trig"], 1)
            for r in range(PAIRS):
                act.wait_ge(s["xs_done"], r + 1)
                A(HN[:, r, :], XS[:, r, 0:D], ACT.Square, accum_out=sm[:, 3, r:r + 1]).then_inc(s["ssq_done"], 1)
            act.wait_ge(s["ssq_done"], PAIRS)
            A(sm[:, 4, 0:PAIRS], sm[:, 3, 0:PAIRS], ACT.Sqrt, bias=cc("eps")[:, 1:2], scale=1.0 / D).then_inc(s["std_done"], 1)
            for r in range(PAIRS):
                act.wait_ge(s["mqkv_ps"], r + 1)
                A(QKV[:, r, :], bank(r)[:, 0:3 * D], ACT.Copy).then_inc(s["mqkv_sb"], 1)
            act.wait_ge(s["vzero"], 1)
            act.wait_ge(s["mqkv_sb"], PAIRS)
            for b in range(B):
                r, hs = b // 2, slice(64 * (b % 2), 64 * (b % 2) + 64)
                v = QKV[hs, r, 2 * D:3 * D].rearrange("p (k o n) -> p k o n", k=8, o=2)
                A(VBD[0:64, b, :, 0:8], v[:, :, 0, :], ACT.Copy)
                A(VBD[64:128, b, :, 8:16], v[:, :, 1, :], ACT.Copy).then_inc(s["vbd_done"], 1)

            def at_copy(r):
                act.wait_ge(s["at_ps"], r + 1)
                if r >= 2:
                    act.wait_ge(s["op_ps"], r - 1)
                o = 4 + 2 * (r % 2)
                A(AT[:, r % 2, :, :].rearrange("p k n -> p (k n)"), PS[:, o:o + 2, :].rearrange("p b n -> p (b n)"),
                  ACT.Copy).then_inc(s["at_sb"], 1)

            for r in range(PAIRS):
                act.wait_ge(s["smx_done"], r + 1)
                act.wait_ge(s["ae_done"], r + 1)
                a = AE[:, r % 2, :, 0:CAP]
                A(a, a, ACT.Exp).then_inc(s["exp_mod"], 1)
                if r >= 1:
                    at_copy(r - 1)
            at_copy(PAIRS - 1)
            for r in range(PAIRS):
                act.wait_ge(s["oot_ps"], r + 1)
                A(OOT[:, r, :], bank(4 + r)[:, 0:128], ACT.Copy).then_inc(s["oot_sb"], 1)
            for r in range(PAIRS):
                act.wait_ge(s["x1s_done"], r + 1)
                A(H2[:, r, :], X1S[:, r, :], ACT.Square, accum_out=sm[:, 5, r:r + 1]).then_inc(s["ssq_done"], 1)
            act.wait_ge(s["ssq_done"], 2 * PAIRS)
            A(sm[:, 6, 0:PAIRS], sm[:, 5, 0:PAIRS], ACT.Sqrt, bias=cc("eps")[:, 1:2], scale=1.0 / D).then_inc(s["std_done"], 1)
            for r in range(PAIRS):
                act.wait_ge(s["ss_ps"], r + 1)
                A(SS[:, r, :, :].rearrange("p c n -> p (c n)"), bank(4 + r), ACT.Copy).then_inc(s["ss_sb"], 1)
            for r in range(PAIRS):
                act.wait_ge(s["h2t_ps"], r + 1)
                A(H2T[:, r, :], bank(4 + r)[:, 0:128], ACT.Copy).then_inc(s["h2t_sb"], 1)
            for r in range(PAIRS):
                act.wait_ge(s["w1_ps"], r + 1)
                A(GT[:, r, :, :].rearrange("p f n -> p (f n)"), bank(4 + r), ACT.Gelu_apprx_tanh).then_inc(s["gelu_done"], 1)

            def os_copy(b, g, first=False):
                act.wait_ge(s["av_done"], at(b, 16, 4 * g + 4))
                if not first:
                    act.wait_ge(s["ot_ps"], at(b, 4, g))
                A(OS0, bank(6), ACT.Copy).then_inc(s["os_done"], 1)

            def std1(first, last):
                act.wait_ge(s["stats_done"], 4 if first == 0 else 5)
                cols = slice(C * first, C * last)
                A(sm[:, 0, cols], mv[:, cols, 1], ACT.Sqrt, bias=cc("eps")[:, 0:1]).then_inc(s["std_done"], 1)

            def steps0(b, first=False, last=False):
                for u in range(16):
                    if not (first and u < 4):
                        act.wait_ge(s["av_done"], at(b, 16, u - 3))
                    if u % 4 == 2 and not (first and u == 2):
                        if u == 2:
                            os_copy(b - 1, 3)
                        else:
                            os_copy(b, u // 4 - 1, first=first and u == 6)
                    for h in range(HG):
                        k = 4 * u + h
                        act.wait_ge(s["st_full"], at(b, 64, k + 1))
                        A(P0[:, u % 4, h, :], bank(4 + k % 2), ACT.Exp, scale=SC0).then_inc(s["exp_done"], 1)
                    if last and u == 10:
                        std1(0, B - 1)

            act.wait_ge(s["scat_ps"], B)
            act.wait_ge(s["pr_done"], PAIRS)
            steps0(0, first=True)
            with act.Fori(1, B - 1) as i:
                steps0(i)
            steps0(B - 1, last=True)
            os_copy(B - 1, 3)

            def gate_copy(b):
                act.wait_ge(s["gtr_ps"], b + 1)
                A(GTT[:, b % 2, :], bank(7)[0:64, :], ACT.Copy).then_inc(s["gtr_sb"], 1)

            def xt1_copy(b):
                act.wait_ge(s["xt2_ps"], b + 1)
                if b >= 2:
                    act.wait_ge(wrx[b % 2], 16 * (b // 2))
                    act.wait_ge(s["cb_ps"], b - 1)
                A(xT1[b % 2], bank(0), ACT.Copy).then_inc(s["xt2_sb"], 1)

            xt1_copy(0)
            std1(B - 1, B)
            for b in range(B):
                p = b % 2
                if b >= 2:
                    act.wait_ge(wr1[p], 16 * 12 * (b // 2))
                for a in range(2):
                    m = 4 * b + 2 * a
                    act.wait_ge(s["qk1_ps"], m + 1)
                    A(pq1[:, p, 0, a, :], bank(1 + m % 3), ACT.Copy).then_inc(s["p1_part1"], 1)
                    act.wait_ge(s["qk1_ps"], m + 2)
                    A(pk1[:, p, 0, a, 0:ENC], bank(4)[:, 128 * a:128 * a + ENC], ACT.Copy)
                    A(pk1[:, p, 0, a, ENC:KEYS], bank(1 + (m + 1) % 3), ACT.Copy).then_inc(s["p1_part1"], 1)
                    for k, (t, n) in enumerate(((pq1, S), (pk1, KEYS))):
                        act.wait_ge(s["p1_rem"], m + k + 1)
                        A(t[:, p, 1, a, :], rem1[:, k, 0:n], ACT.Copy).then_inc(s["part2"], 1)
                    if a == 0 and b:
                        gate_copy(b - 1)
                if b + 1 < B:
                    xt1_copy(b + 1)
                act.wait_ge(s["lmax_done"], b + 1)
                A(LG[:, 1], LG[:, 0], ACT.Exp).then_inc(s["lexp"], 1)
            gate_copy(B - 1)

            def sq(b, g, h, pieces, first=False):
                if first and g == 1 and h == 0 and pieces[0] == 0:
                    for p in range(2):
                        act.wait_ge(wr1[p], 16 * 12 * (B // 2))
                if h == 0 and pieces[0] == 0 and not (first and g < 2):
                    act.wait_ge(s["den_ps"], at(b, 4, g - 1))
                for k in pieces:
                    o, n = ((BLK_O[0], BLK_N[0]), (BLK_O[1], BLK_N[1]), (BLK_O[2], BLK_N[2] + BLK_N[3]), (BLK_O[4], BLK_N[4]))[k]
                    m = 16 * g + 4 * h + k
                    act.wait_ge(s["sf1"], at(b, 64, m + 1))
                    A(P1[:, g % 2, h, o:o + n], bank((4 * h + k) % 3)[:, 0:n], ACT.Square, scale=0.25, bias=cc("eps")[:, 3:4]
                      ).then_inc(s["sq1d"], 1)

            def v_copy(b, g, k):
                act.wait_ge(s["v1_ps"], at(b, 12, 3 * g + k + 1))
                if k < 2:
                    A(V1[:, g, 2 * k:2 * k + 2, :].rearrange("p j n -> p (j n)"), bank(6), ACT.Copy).then_inc(s["v1_cp"], 1)
                else:
                    A(V1[0:64, g, 4, :], PS[0:64, 6, 0:256], ACT.Copy).then_inc(s["v1_cp"], 1)

            def steps1(b, first=False, last=False):
                for g in range(G):
                    for h in range(HG):
                        vn = (b if g < 3 else b + 1, (g + 1) % G) if h > 1 and not (last and g == 3) else None
                        sq(b, g, h, (0, 1), first)
                        if vn:
                            v_copy(*vn, h - 2)
                        sq(b, g, h, (2, 3), first)
                        if vn and h == 3:
                            v_copy(*vn, 2)
                    if g == 2 and not last:
                        nb = b + 1
                        src = sx1[nb] if isinstance(nb, int) else sx1[bass.ds(nb, 1)].rearrange("o p n -> (o p) n")
                        act.dma_start(xTc, src).then_inc(xt_in, 16)

            for k in range(3):
                v_copy(0, 0, k)
            act.wait_ge(s["x1_l1"], B)
            steps1(0, first=True)
            with act.Fori(1, B - 1) as i:
                steps1(i)
            steps1(B - 1, last=True)

        @block.vector
        def _(dve):
            v = nc.vector
            chain = [0]

            def link(ins):
                chain[0] += 1
                ins.then_inc(s["chain_v"], 1)
                dve.wait_ge(s["chain_v"], chain[0])

            def inv_sqrt(var, eps, scale, std, done, n):
                o = sm[:, 2, n]
                t = sm[:, 7, n]
                link(v.reciprocal(o, std))
                link(v.tensor_scalar(t, var, scale, eps, ALU.mult, ALU.add))
                link(v.tensor_tensor(t, t, o, ALU.mult))
                link(v.tensor_tensor(t, t, o, ALU.mult))
                link(v.tensor_scalar(t, t, -0.5, 1.5, ALU.mult, ALU.add))
                v.tensor_tensor(o, o, t, ALU.mult).then_inc(done, 1)

            def moments0(first, last):
                for b in range(first, last):
                    if b % 2 == 0:
                        dve.wait_ge(x_in[b // 2], 32)
                    for c in range(C):
                        ins = v.bn_stats(st6[:, C * b + c, :], X1[:, C * b + c, :])
                link(ins)
                for t in range(C * first, C * last):
                    ins = v.bn_aggr(mv[:, t, :], st6[:, t, :])
                k = 1 if first == 0 else 2
                ins.then_inc(s["stats_done"], 1)
                dve.wait_ge(s["stats_done"], k)
                dve.wait_ge(s["std_done"], k)
                cols = slice(C * first, C * last)
                inv_sqrt(mv[:, cols, 1], LN_EPS, 1.0, sm[:, 0, cols], s["rstd_done"], cols)
                dve.wait_ge(s["rstd_done"], k)

            moments0(0, 2)

            def norm0(b):
                for t in range(C * b, C * b + C):
                    ins = v.tensor_scalar(XN[:, t, 0:D], X1[:, t, :], mv[:, t, 0:1], sm[:, 2, t:t + 1], ALU.subtract, ALU.mult)
                ins.then_inc(s["xn_done"], 1)

            norm0(0)
            norm0(1)
            moments0(2, B)
            for p in range(RING):
                link(v.memset(vb0[p].rearrange("p g c h n -> p (g c h n)"), 1.0))
            dve.wait_ge(s["rows_in"], 16)
            def vps():
                return PS[:, 6:8, :].rearrange("p b (c n) -> p (b c) n", c=2)

            for b in range(B):
                p = b % RING
                if b + 2 < B:
                    norm0(b + 2)
                dve.wait_ge(s["v_ps"], b + 1)
                if b >= RING:
                    dve.wait_ge(wr0[p], 16 * 7 * (b // RING))
                vv = rr("vb").rearrange("p (g h n) -> p g h n", g=G, h=HG)
                for g in range(G):
                    ins = v.tensor_tensor(vb0[p][:, g, :, :, 0:8],
                                          vps()[:, :, 32 * g:32 * g + 32].rearrange("p c (h n) -> p c h n", h=HG),
                                          vv[:, g].unsqueeze(1).to_broadcast([128, C, HG, 8]), ALU.add)
                ins.then_inc(s["v_sb"], 1)
                v.tensor_scalar(WT[:, C * b:C * b + C], vps()[:, :, D], rr("mrb"), None, ALU.add).then_inc(s["wt_done"], 1)
                for k in range(2):
                    dve.wait_ge(s["part1"], 2 * b + k + 1)
                    if b:
                        dve.wait_ge(s["part3"], 2 * b + k - 1)
                    v.scalar_tensor_tensor(out=rem0[:, k, :], in0=bank(2 + 2 * (b % 2) + k), scalar=rr("qkb")[:, k:k + 1],
                                           in1=part0[p][:, k, 0, :], op0=ALU.add, op1=ALU.subtract).then_inc(s["rem_done"], 1)
            dve.wait_ge(s["wt_ps"], 1)
            v.tensor_copy(wrow, bank(0)[0:32, 0:128]).then_inc(s["wt_row"], 1)
            dve.wait_ge(s["pos_in"], 16)
            TWO_PI = 2 * np.pi
            C1, C2 = 6.28125, float(np.float32(0.0019350051879882812))
            C3 = TWO_PI - C1 - C2
            posf = sm[:, 1, 0:MB * C]
            link(v.tensor_copy(posf, posi[:]))
            inv = (np.float32(1.0) / np.float32(10000.0) ** (np.arange(0, HD0, 2, dtype=np.float32) / np.float32(HD0)))
            f4 = ang[:, 0, :].rearrange("p (n j) -> p n j", j=4)
            for j in range(4):
                link(v.tensor_scalar(f4[:, :, j], posf, float(inv[j]), None, ALU.mult))
            MAGIC = 12582912.0
            link(v.tensor_scalar(ang[:, 1, :], ang[:, 0, :], 1.0 / TWO_PI, MAGIC, ALU.mult, ALU.add))
            link(v.tensor_scalar(ang[:, 1, :], ang[:, 1, :], MAGIC, None, ALU.subtract))
            for k in (C1, C2, C3):
                link(v.scalar_tensor_tensor(out=ang[:, 0, :], in0=ang[:, 1, :], scalar=-k, in1=ang[:, 0, :], op0=ALU.mult,
                                            op1=ALU.add))
            link(v.tensor_scalar(ang[:, 0, :], ang[:, 0, :], 3.1415925, -3.1415925, ALU.min, ALU.max))
            link(v.tensor_scalar(ang[:, 1, :], ang[:, 0, :], -1.0, None, ALU.mult))
            link(v.tensor_tensor(ang[:, 1, :], ang[:, 0, :], ang[:, 1, :], ALU.max))
            v.tensor_scalar(ang[:, 1, :], ang[:, 1, :], -1.0, float(np.pi / 2), ALU.mult, ALU.add).then_inc(s["trig_r"], 1)

            dve.wait_ge(s["trig"], 1)
            a4 = ang.rearrange("p a (b c j) -> p a b c j", b=MB, c=C)
            for b in range(B):
                m = min(b, MB - 1)
                v.tensor_copy(XN[:, C * b:C * b + C, D:D + 4], a4[:, 3, m])
                v.tensor_copy(XN[:, C * b:C * b + C, D + 4:D + 8], a4[:, 2, m])
            v.tensor_copy(XN[:, :, D + 8], WT[:])
            v.tensor_copy(XN[:, :, D + 9], cc("token")).then_inc(s["trig_done"], 1)

            link(v.memset(RS, 0.0))
            link(v.memset(m8[:], 0.0))
            dve.wait_ge(s["wrow_moved"], 32)
            link(v.tensor_copy(SEL[:, 1, :], SEL[:, 0, :]))
            for k in range(8):
                link(v.max(m8[:, 0:8], SEL[:, 1, :]))
                if k == 7:
                    link(v.tensor_copy(m8[:, 8:9], m8[:, 7:8]))
                    link(v.memset(m8[:, 7:8], NEG))
                link(v.match_replace(out=SEL[:, 1, :], in_to_replace=m8[:, 0:8], in_values=SEL[:, 1, :], imm_value=NEG))
            link(v.tensor_scalar(RS[32:32 + B, :], SEL[:, 0, :], m8[:, 8:9], None, ALU.is_le))
            link(v.tensor_scalar(SEL[:, 1, :], SEL[:, 1, :], NEG, None, ALU.is_equal))
            link(v.tensor_tensor_scan(RS[0:B, :], SEL[:, 1, :], SEL[:, 1, :], 0.0, ALU.add, ALU.max))
            v.tensor_tensor(RS[0:B, :], RS[0:B, :], SEL[:, 1, :], ALU.mult).then_inc(s["rs_done"], 1)
            dve.wait_ge(s["rs_ps"], 1)
            for p in range(RING):
                dve.wait_ge(wr0[p], 16 * 7 * (B // RING))
            v.tensor_copy(TS.rearrange("p c n -> p (c n)"), bank(1)[:, 0:96 * C]).then_inc(s["ts_done"], 1)
            dve.wait_ge(s["ts_done"], 1)
            for r in range(PAIRS):
                v.tensor_tensor(ST[:, r].rearrange("p c (k n) -> p c k n", k=2),
                                cc("iota").unsqueeze(1).unsqueeze(1).to_broadcast([128, C, 2, SLOT]),
                                TS[:, :, 2 * r:2 * r + 2].unsqueeze(3).to_broadcast([128, C, 2, SLOT]), ALU.is_equal
                                ).then_inc(s["onehot"], 1)
            link(v.memset(VBD.rearrange("p b k n -> p (b k n)"), 0.0))
            v.memset(AE.rearrange("p s h n -> p (s h n)"), 0.0).then_inc(s["vzero"], 1)
            for r in range(PAIRS):
                dve.wait_ge(s["g_ps"], r + 1)
                v.tensor_copy(XS[:, r, :], bank(r)[:, 0:XW]).then_inc(s["xs_done"], 1)
            dve.wait_ge(s["xs_done"], PAIRS)
            v.tensor_tensor(idx[:], XS[:, :, D + 9], cc("off"), ALU.add).then_inc(s["idx_done"], 1)
            dve.wait_ge(s["std_done"], 3)
            inv_sqrt(sm[:, 3, 0:PAIRS], RMS_EPS, 1.0 / D, sm[:, 4, 0:PAIRS], s["rstd_done"], slice(0, PAIRS))
            dve.wait_ge(s["rstd_done"], 3)
            for r in range(PAIRS):
                v.scalar_tensor_tensor(out=HN[:, r, :], in0=XS[:, r, 0:D], scalar=sm[:, 2, r:r + 1], in1=rr("ln1"),
                                       op0=ALU.mult, op1=ALU.mult).then_inc(s["hn_done"], 1)
            for r in range(PAIRS):
                dve.wait_ge(s["ht_ps"], r + 1)
                v.tensor_copy(HT[:, r, :], bank(4 + r)[:, 0:128]).then_inc(s["ht_sb"], 1)
            for r in range(PAIRS):
                dve.wait_ge(s["mqkv_sb"], r + 1)
                qk = QKV[:, r, 0:2 * D].rearrange("p (h n) -> p h n", n=4)
                xc, xs_ = (AB[:, a, :].rearrange("p (h n) -> p h n", n=4) for a in range(2))
                cosb, sinb = (XS[:, r, D + 4 * a:D + 4 * a + 4].unsqueeze(1).to_broadcast([128, 4 * H, 4]) for a in range(2))
                if r:
                    dve.wait_ge(s["rope_done"], r)
                v.tensor_tensor(xc, qk, cosb, ALU.mult)
                link(v.tensor_tensor(xs_, qk, sinb, ALU.mult))
                xc2, xs2, o2 = (t.rearrange("p (h o n) -> p h o n", o=2, n=4)
                                for t in (AB[:, 0, :], AB[:, 1, :], RQ[:, r, :]))
                v.tensor_tensor(o2[:, :, 0, :], xc2[:, :, 0, :], xs2[:, :, 1, :], ALU.subtract)
                v.tensor_tensor(o2[:, :, 1, :], xc2[:, :, 1, :], xs2[:, :, 0, :], ALU.add).then_inc(s["rope_done"], 1)
            for r in range(PAIRS):
                dve.wait_ge(s["mr_ps"], r + 1)
                v.tensor_scalar(MRT[:, r].rearrange("p c n -> p (c n)"), bank(r), FMIN, None, ALU.max).then_inc(s["mrt_done"], 1)
            for r in range(PAIRS):
                dve.wait_ge(s["rt_ps"], r + 1)
                v.tensor_copy(RQ[:, r, :], bank(4 + r)[:, 0:2 * D]).then_inc(s["qt_done"], 1)

            def softmax_in(r):
                dve.wait_ge(s["sc_ps"], 2 * r + 2)
                if r >= 2:
                    dve.wait_ge(s["at_ps"], r - 1)
                a = AE[:, r % 2, :, 0:CAP]
                for k in range(2):
                    ins = v.scalar_tensor_tensor(out=AE[:, r % 2, 8 * k:8 * k + 8, 0:CAP],
                                           in0=bank(2 * (r % 2) + k).rearrange("p (h n) -> p h n", h=8)[:, :, 0:CAP],
                                           scalar=SC0, in1=MS[:, r, 0:CAP].unsqueeze(1).to_broadcast([128, 8, CAP]),
                                           op0=ALU.mult, op1=ALU.add)
                ins.then_inc(s["smx_done"], 1)
                dve.wait_ge(s["smx_done"], r + 1)
                link(v.tensor_reduce(am[:, 0, r, :], a, AX.X, ALU.max))
                v.tensor_tensor(a, a, am[:, 0, r, :].unsqueeze(2).to_broadcast([128, H, CAP]), ALU.subtract
                                ).then_inc(s["ae_done"], 1)

            def softmax_sum(r):
                dve.wait_ge(s["exp_mod"], r + 1)
                link(v.tensor_reduce(am[:, 1, r, :], AE[:, r % 2, :, 0:CAP], AX.X, ALU.add))
                link(v.reciprocal(am[:, 2, r, :], am[:, 1, r, :]))

            for r in range(PAIRS):
                dve.wait_ge(s["ms_ps"], r + 1)
                v.tensor_copy(MS[:, r, :], bank(r)[:, 0:SLOT]).then_inc(s["ms_done"], 1)
            dve.wait_ge(s["ms_done"], PAIRS)
            softmax_in(0)
            softmax_in(1)
            softmax_sum(0)
            softmax_in(2)
            softmax_sum(1)
            softmax_in(3)
            softmax_sum(2)
            softmax_sum(3)
            for r in range(PAIRS):
                dve.wait_ge(s["op_ps"], r + 1)
                v.tensor_tensor(OO[:, r, :].rearrange("p (h n) -> p h n", h=H),
                                bank(r)[:, 0:D].rearrange("p (h n) -> p h n", h=H),
                                am[:, 2, r, :].unsqueeze(2).to_broadcast([128, H, HD0]), ALU.mult).then_inc(s["oo_done"], 1)
            def mt_copy(n, p, src=bank(7)):
                dve.wait_ge(s["mt_ps"], n + 1)
                v.tensor_scalar(mT[:, p, :], src[0:16, 0:128], -1.0, None, ALU.mult).then_inc(s["mt_sb"], 1)

            def smax(n, p, h, slots=(0, 1)):
                for k in slots:
                    dve.wait_ge(s["s_full"], n * 2 + k + 1)
                    v.tensor_reduce(mx[:, p, 4 * h + 2 * k:4 * h + 2 * k + 2], PS[:, 2 * k:2 * k + 2, :], AX.X, ALU.max
                                    ).then_inc(s["s_free"], 1)

            smax(0, 0, 0)
            for r in range(PAIRS):
                dve.wait_ge(s["wo_ps"], r + 1)
                v.tensor_tensor(X1S[:, r, :], XS[:, r, 0:D], bank(4 + r)[:, D:2 * D], ALU.add).then_inc(s["x1s_done"], 1)
            smax(1, 0, 1)
            dve.wait_ge(s["std_done"], 4)
            inv_sqrt(sm[:, 5, 0:PAIRS], RMS_EPS, 1.0 / D, sm[:, 6, 0:PAIRS], s["rstd_done"], slice(0, PAIRS))
            dve.wait_ge(s["rstd_done"], 4)
            for r in range(PAIRS):
                v.scalar_tensor_tensor(out=H2[:, r, :], in0=X1S[:, r, :], scalar=sm[:, 2, r:r + 1], in1=rr("ln2"),
                                       op0=ALU.mult, op1=ALU.mult).then_inc(s["h2_done"], 1)
            for h in range(2, 6):
                smax(h, h // 4, h % 4)
            for r in range(PAIRS):
                dve.wait_ge(s["w2_ps"], r + 1)
                link(v.tensor_tensor(PR[:, r, :], X1S[:, r, :], bank(4 + r)[:, 256:384], ALU.add))
                v.tensor_scalar(PR[:, r, :], PR[:, r, :], XS[:, r, D + 8:D + 9], None, ALU.mult).then_inc(s["pr_done"], 1)
            smax(6, 1, 2)
            mt_copy(0, 0, bank(3))
            for b in range(B):
                if b == 4:
                    smax(7, 1, 3)
                dve.wait_ge(s["scat_ps"], b + 1)
                dve.wait_ge(s["x1b_done"], b + 1)
                for c in range(C):
                    t = C * b + c
                    ins = v.scalar_tensor_tensor(out=XN[:, t, 0:D], in0=XN[:, t, 0:D], scalar=TS[:, c, 32 + b:33 + b],
                                                 in1=bank(4 + b % 4)[:, 128 * c:128 * c + 128], op0=ALU.mult, op1=ALU.add)
                ins.then_inc(s["ffn_done"], 1)

            def normal(b, g):
                dve.wait_ge(s["ot_ps"], at(b, 4, g + 1))
                o = bank(7).rearrange("p (c h n) -> p c h n", c=C, h=HG)
                v.reciprocal(rd0, o[:, :, :, 8]).then_inc(s["rd_done"], 1)
                dve.wait_ge(s["rd_done"], at(b, 4, g + 1))
                v.tensor_tensor(OQ0[:, :, 32 * g:32 * g + 32].rearrange("p c (h n) -> p c h n", h=HG), o[:, :, :, 0:8],
                                rd0.unsqueeze(3).to_broadcast([128, C, HG, 8]), ALU.mult).then_inc(s["oq_done"], 1)

            def ot_copy(b):
                dve.wait_ge(s["otT_ps"], b + 1)
                v.tensor_copy(OT0, bank(7)).then_inc(s["otT_sb"], 1)

            def residual(b):
                dve.wait_ge(s["proj_ps"], b + 1)
                dst = X1[:, C * b:C * b + C, :] if isinstance(b, int) else X1[:, bass.ds(b * C, C), :]
                v.tensor_tensor(dst, dst, bank(7).rearrange("p (c n) -> p c n", c=C), ALU.add).then_inc(s["x1_l0"], 1)

            def stats1(b):
                dve.wait_ge(s["x1_l0"], b + 1)
                for c in range(C):
                    if isinstance(b, int):
                        ins = v.bn_stats(st6[:, C * b + c, :], X1[:, C * b + c, :])
                    else:
                        t = bass.ds(b * C + c, 1)
                        ins = v.bn_stats(st6[:, t, :].rearrange("p o n -> p (o n)"), X1[:, t, :].rearrange("p o n -> p (o n)"))
                return ins

            def norms1(first, last):
                if last == B:
                    link(stats1(B - 1))
                else:
                    dve.wait_ge(s["stats_done"], 3)
                for t in range(C * first, C * last):
                    ins = v.bn_aggr(mv[:, t, :], st6[:, t, :])
                ins.then_inc(s["stats_done"], 1)
                k = 0 if first == 0 else 1
                dve.wait_ge(s["stats_done"], 4 + k)
                dve.wait_ge(s["std_done"], 5 + k)
                cols = slice(C * first, C * last)
                inv_sqrt(mv[:, cols, 1], LN_EPS, 1.0, sm[:, 0, cols], s["rstd_done"], cols)
                dve.wait_ge(s["rstd_done"], 5 + k)

            def norm1(b):
                if b >= 2:
                    dve.wait_ge(s["xt2_ps"], b - 1)
                for c in range(C):
                    t = C * b + c
                    ins = v.tensor_scalar(xb1[b % 2][:, c, :], X1[:, t, :], mv[:, t, 0:1], sm[:, 2, t:t + 1], ALU.subtract,
                                          ALU.mult)
                ins.then_inc(s["xb_done"], 1)

            def steps0(b, first=False, last=False):
                for u in range(16):
                    g, kc = u // 4, u % 4
                    if u == 7 and not first:
                        ins = stats1(b - 1)
                        if last:
                            ins.then_inc(s["stats_done"], 1)
                    if last and u == 9:
                        norms1(0, B - 1)
                        norm1(0)
                        norm1(1)
                    if u == 5 and not first:
                        ot_copy(b - 1)
                    if u == 6 and not first:
                        residual(b - 1)
                    if not (last and u >= 8):
                        u2 = (u + 8) % 16
                        nb = b if u < 8 else b + 1
                        smax(at(nb, 16, u2), (u2 // 4) % 2, u2 % 4, (0,))
                    if kc == 0 and not (last and g == 3):
                        mt_copy(at(b, 4, g + 1), (g + 1) % 2)
                    if not (last and u >= 8):
                        smax(at(nb, 16, u2), (u2 // 4) % 2, u2 % 4, (1,))
                    if kc == 2 and not (first and g == 0):
                        if g == 0:
                            normal(b - 1, 3)
                        else:
                            normal(b, g - 1)

            dve.wait_ge(s["ffn_done"], B)
            v.memset(bank(6), 0.0).then_inc(s["av_zero"], 1)
            steps0(0, first=True)
            dve.wait_ge(s["mod_x1"], B)
            with dve.Fori(1, B - 1) as i:
                steps0(i)
            steps0(B - 1, last=True)
            normal(B - 1, 3)
            ot_copy(B - 1)
            residual(B - 1)

            norms1(B - 1, B)

            def add_lora(b):
                dve.wait_ge(s["lora_ps"], b + 1)
                xo = X1[:, C * b:C * b + C, :]
                v.tensor_tensor(xo, xo, bank(7).rearrange("p (c n) -> p c n", c=C), ALU.add).then_inc(s["x1_l1"], 1)

            def cps():
                return PS[:, 5:7, :].rearrange("p b (c n) -> p (b c) n", c=2)

            for b in range(B):
                p = b % 2
                if b + 2 < B:
                    norm1(b + 2)
                for a in range(2):
                    m = 4 * b + 2 * a
                    dve.wait_ge(s["p1_part1"], m + 1)
                    if m >= 2:
                        dve.wait_ge(s["p1_part3"], m - 1)
                    v.tensor_tensor(rem1[:, 0, 0:S], bank(1 + m % 3), pq1[:, p, 0, a, :], ALU.subtract).then_inc(s["p1_rem"], 1)
                    dve.wait_ge(s["p1_part1"], m + 2)
                    if m >= 2:
                        dve.wait_ge(s["p1_part3"], m)
                    v.tensor_tensor(rem1[:, 1, 0:ENC], bank(4)[:, 128 * a:128 * a + ENC], pk1[:, p, 0, a, 0:ENC], ALU.subtract)
                    v.tensor_tensor(rem1[:, 1, ENC:KEYS], bank(1 + (m + 1) % 3), pk1[:, p, 0, a, ENC:KEYS], ALU.subtract
                                    ).then_inc(s["p1_rem"], 1)
                dve.wait_ge(s["cb_ps"], b + 1)
                link(v.tensor_tensor(LG[:, 2], cps()[:, :, D:D + E], rr("rb").unsqueeze(1).to_broadcast([128, C, E]), ALU.add))
                link(v.tensor_reduce(lmx[:, 0, :], LG[:, 2], AX.X, ALU.max))
                v.tensor_tensor(LG[:, 0], LG[:, 2], lmx[:, 0, :].unsqueeze(2).to_broadcast([128, C, E]), ALU.subtract
                                ).then_inc(s["lmax_done"], 1)
                xo = X1[:, C * b:C * b + C, :]
                dve.wait_ge(s["base_done"], b + 1)
                link(v.tensor_tensor(xo, xo, cps()[:, :, 0:D], ALU.add))
                dve.wait_ge(s["lexp"], b + 1)
                link(v.tensor_reduce(lmx[:, 1, :], LG[:, 1], AX.X, ALU.add))
                link(v.reciprocal(lmx[:, 2, :], lmx[:, 1, :]))
                link(v.tensor_tensor(GB, LG[:, 1], lmx[:, 2, :].unsqueeze(2).to_broadcast([128, C, E]), ALU.mult))
                for c in range(C):
                    ins = v.scalar_tensor_tensor(out=GM[:, p, c, :].rearrange("p (e r) -> p e r", e=E),
                                                 in0=GB[:, c, :].unsqueeze(2).to_broadcast([128, E, R]), scalar=2.0,
                                                 in1=cps()[:, c, D + E:D + E + R].unsqueeze(1).to_broadcast([128, E, R]),
                                                 op0=ALU.mult, op1=ALU.mult)
                ins.then_inc(s["gm_done"], 1)
                if b:
                    add_lora(b - 1)
            add_lora(B - 1)
            dve.wait_ge(s["x1_l1"], B)
            v.memset(bank(5), 0.0).then_inc(s["l1_zero"], 1)
            v.memset(V1[64:128, :, 4, :], 0.0).then_inc(s["l1_zero"], 1)

            def masked(b, g, h):
                dve.wait_ge(s["sq1d"], at(b, 64, 16 * g + 4 * h + 4))
                pv = P1[:, g % 2, h, :]
                v.scalar_tensor_tensor(out=pv, in0=pv, scalar=1.0, in1=cc("keep"), op0=ALU.add, op1=ALU.mult
                                       ).then_inc(s["mask1"], 1)

            def first_sum(b, g, h):
                dve.wait_ge(s["mask1"], at(b, 16, 4 * g + h + 1))
                q, pv = BLK_Q[1], P1[:, g % 2, h, :]
                v.tensor_tensor(PSUMS[:, g % 2, h, q:S], pv[:, q:S], pv[:, BLK_O[1]:BLK_O[1] + BLK_N[1]], ALU.add
                                ).then_inc(s["sum_first"], 1)

            def y_copy(b, g, a, p, free):
                dve.wait_ge(s["y_ps"], at(b, 8, 2 * g + a + 1))
                if free is not None:
                    dve.wait_ge(s["wout_ps"], free)
                v.tensor_copy(Y1[:, p, a, :], bank(3 + a)).then_inc(s["y_cp"], 1)

            def den_copy(b, g, p):
                dve.wait_ge(s["den_ps"], at(b, 4, g + 1))
                v.tensor_copy(dn1[:, p, :], bank(5)).then_inc(s["den_cp"], 1)

            def recip(b, g, p):
                dve.wait_ge(den_in, at(b, 64, 16 * g + 16))
                v.reciprocal(zR[:, p, :], dR[:, p, :]).then_inc(s["rec1"], 1)

            def add_out(b):
                dve.wait_ge(s["wout_ps"], at(b, 4, 4))
                dst = X1[:, C * b:C * b + C, :] if isinstance(b, int) else X1[:, bass.ds(b * C, C), :]
                v.tensor_tensor(dst, dst, bank(7).rearrange("p (c n) -> p c n", c=C), ALU.add).then_inc(s["out_add"], 1)

            def prev(b, g, k):
                return (b, g - k) if g >= k else (b - 1, g - k + G)

            def steps1(b, first=False, last=False):
                for g in range(G):
                    p = (g - 1) % 2
                    masked(b, g, 0)
                    if not (first and g < 2):
                        recip(*prev(b, g, 2), g % 2)
                    first_sum(b, g, 0)
                    masked(b, g, 1)
                    if g == 2 and not first:
                        add_out(b - 1)
                    first_sum(b, g, 1)
                    for a in range(2):
                        if not (first and g == 0):
                            y_copy(*prev(b, g, 1), a, p, None if first and g < 3 else at(b, 4, g - 2))
                        masked(b, g, 2 + a)
                    if not (first and g == 0):
                        den_copy(*prev(b, g, 1), p)
                    first_sum(b, g, 2)
                    first_sum(b, g, 3)

            dve.wait_ge(s["keep_in"], 16)
            dve.wait_ge(s["p1_part3"], 4 * B)
            for p in range(2):
                dve.wait_ge(wrx[p], 16 * (B // 2))
            steps1(0, first=True)
            with dve.Fori(1, B - 1) as i:
                steps1(i)
            steps1(B - 1, last=True)
            recip(B - 1, 2, 0)
            den_copy(B - 1, 3, 1)
            y_copy(B - 1, 3, 0, 1, 30)
            recip(B - 1, 3, 1)
            y_copy(B - 1, 3, 1, 1, 30)
            add_out(B - 1)

        @block.gpsimd
        def _(pool):
            g_ = nc.gpsimd
            for t in (KS, QS):
                g_.memset(t[:].rearrange("p g h n -> p (g h n)").bitcast(F32), 0.0).then_inc(s["ks_zero"], 1)
            pool.wait_ge(s["rows_in"], 16)
            for b in range(B):
                for k in range(2):
                    pool.wait_ge(s["part2"], 2 * b + k + 1)
                    g_.tensor_tensor(part0[b % RING][:, k, 2, :], rem0[:, k, :], part0[b % RING][:, k, 1, :], ALU.subtract
                                     ).then_inc(s["part3"], 1)
            pool.wait_ge(s["xn_done"], B)
            for b in range(B):
                xo = X1[:, C * b:C * b + C, :]
                g_.tensor_tensor(xo, xo, rr("projb").unsqueeze(1).to_broadcast([128, C, D]), ALU.add).then_inc(s["x1b_done"], 1)
            pool.wait_ge(s["idx_done"], 1)
            for r in range(PAIRS):
                g_.indirect_dma_start(out=MR[:, r, :], out_offset=None, in_=mask,
                                      in_offset=bass.IndirectOffsetOnAxis(ap=idx[:, r:r + 1], axis=0)).then_inc(mr_in, 16)
            for b in range(B):
                pool.wait_ge(s["qt_done"], b // 2 + 1)
                if b >= 2:
                    pool.wait_ge(s["sc_ps"], b - 1)
                o = 128 + 64 * (b % 2)
                g_.tensor_tensor(KBD[:, b % 2], RQ[:, b // 2, o:o + 64].unsqueeze(1).to_broadcast([128, H, SLOT]),
                                 cc("head").unsqueeze(2).to_broadcast([128, H, SLOT]), ALU.mult).then_inc(s["kbd_done"], 1)

            one16 = cc("eps")[0:16, 3:4].to_broadcast([16, 128])

            def parts(n, p, first):
                pool.wait_ge(s["mt_sb"], n + 1)
                if not first:
                    pool.wait_ge(ext[p], (n * 24 - 24 * p) if not isinstance(n, int) else 48 * (n // 2))
                g_.tensor_tensor(mN[p][:, 0, :], mT[:, p, :], one16, ALU.mult).then_inc(s["chain_p"], 1)
                pool.wait_ge(s["chain_p"], n * 3 + 1)
                g_.tensor_tensor(mR, mT[:, p, :], mN[p][:, 0, :], ALU.subtract).then_inc(s["chain_p"], 1)
                pool.wait_ge(s["chain_p"], n * 3 + 2)
                g_.tensor_tensor(mN[p][:, 1, :], mR, one16, ALU.mult).then_inc(s["chain_p"], 1)
                pool.wait_ge(s["chain_p"], n * 3 + 3)
                g_.tensor_tensor(mN[p][:, 2, :], mR, mN[p][:, 1, :], ALU.subtract).then_inc(s["mn_done"], 1)
                pool.wait_ge(s["mn_done"], n + 1)

            parts(0, 0, True)
            for b in range(B):
                pool.wait_ge(s["ffn_done"], b + 1)
                xo = X1[:, C * b:C * b + C, :]
                g_.tensor_tensor(xo, xo, XN[:, C * b:C * b + C, 0:D], ALU.add).then_inc(s["mod_x1"], 1)
            for n in range(1, 4):
                parts(n, n % 2, n < 2)
            with pool.Fori(1, B) as i:
                for g in range(G):
                    parts(at(i, 4, g), g % 2, False)

            for b in range(B):
                p = b % 2
                pool.wait_ge(s["xb_done"], b + 1)
                xo = X1[:, C * b:C * b + C, :]
                g_.tensor_tensor(xo, xo, rr("baseb").unsqueeze(1).to_broadcast([128, C, D]), ALU.add).then_inc(s["base_done"], 1)
                for a in range(2):
                    for k in range(2):
                        m = 4 * b + 2 * a + k
                        t, n = ((pq1, S), (pk1, KEYS))[k]
                        pool.wait_ge(s["part2"], 2 * B + m + 1)
                        g_.tensor_tensor(t[:, p, 2, a, :], rem1[:, k, 0:n], t[:, p, 1, a, :], ALU.subtract
                                         ).then_inc(s["p1_part3"], 1)

            def scale_y(n, p):
                pool.wait_ge(z_in, n * 64 + 64)
                for a in range(2):
                    pool.wait_ge(s["y_cp"], n * 2 + a + 1)
                    g_.tensor_tensor(Y1[:, p, a, :], Y1[:, p, a, :], Z1[:, p, a, :], ALU.mult).then_inc(s["yn1"], 1)

            def block_sums(b, g, a):
                pool.wait_ge(s["sum_first"], at(b, 16, 4 * g + 2 * a + 2))
                hs = slice(2 * a, 2 * a + 2)
                for k, j in enumerate((2, 3, 4)):
                    if k:
                        pool.wait_ge(s["sum_done"], at(b, 24, 6 * g + 3 * a + k))
                    acc = PSUMS[:, g % 2, hs, BLK_Q[j]:S]
                    g_.tensor_tensor(acc, acc, P1[:, g % 2, hs, BLK_O[j]:BLK_O[j] + BLK_N[j]], ALU.add
                                     ).then_inc(s["sum_done"], 1)

            def steps1(b, first=False):
                for g in range(G):
                    block_sums(b, g, 0)
                    if not (first and g < 2):
                        scale_y(at(b, 4, g - 2), g % 2)
                    block_sums(b, g, 1)

            steps1(0, first=True)
            with pool.Fori(1, B) as i:
                steps1(i)
            for n in (B * G - 2, B * G - 1):
                scale_y(n, n % 2)


_OUT = ((B, S, D), "float32")


def kernel(**inputs):
    import concourse.bacc as _bacc
    from concourse import mybir as _mybir
    from concourse.bass_utils import run_bass_kernel_spmd as _run

    def a(name):
        return np.asarray(inputs[name])

    def wide(v):
        return np.broadcast_to(v.reshape(1, -1), (128, v.size))

    qkv = a("L0_attn_qkv_w")
    qkb = a("L0_attn_qkv_b")
    w0 = np.concatenate([qkv[:, 0:D], qkv[:, D:2 * D], qkv[:, 2 * D:], a("L0_ffn_router_w"), a("L0_attn_proj_w"),
                         a("L0_ffn_wq"), a("L0_ffn_wk"), a("L0_ffn_wv"), a("L0_ffn_wo"), a("L0_ffn_w1"),
                         a("L0_ffn_w2").reshape(F // 128, 128, D).transpose(1, 0, 2).reshape(128, F)], axis=1)
    w1 = np.concatenate([a("L1_attn_Wq").T, a("L1_attn_Wk").T, a("L1_attn_Wk_enc").T, a("L1_attn_Wv").T,
                         a("L1_attn_Wv_enc").T,
                         a("L1_attn_Wout").T.reshape(H // 2, 128, D).transpose(1, 0, 2).reshape(128, H * HD1),
                         a("L1_ffn_base_w").T, a("L1_ffn_router_w").T, a("L1_ffn_lora_A")], axis=1)
    rows = np.concatenate([wide(qkb[2 * D:]), wide(a("L0_attn_proj_b")), wide(a("L1_ffn_base_b")), wide(a("L0_ffn_ln1")),
                           wide(a("L0_ffn_ln2")), wide(a("L1_ffn_router_b")), wide(a("L0_ffn_router_b")),
                           qkb[0:2 * D].reshape(2, D).T], axis=1)
    arrays = {
        "x": a("L0_attn_x"), "consts": constants(), "rows": rows, "w0": w0, "w1": w1,
        "lora_b": a("L1_ffn_lora_B").reshape(E * R, D), "mask": a("L0_ffn_attention_mask").reshape(MB * S, S),
        "pos": a("L0_ffn_position_ids").reshape(MB * C, 128).T, "ones_rows": np.ones((3, G, HG, KPAD), _mybir.dt.np(BF16)),
    }
    arrays = {f"in_{k}": np.ascontiguousarray(v) for k, v in arrays.items()}
    nc = _bacc.Bacc("TRN2", target_bir_lowering=False, num_devices=1)
    args = [nc.dram_tensor(k, v.shape, _mybir.dt.from_np(v.dtype), kind="ExternalInput").ap() for k, v in arrays.items()]
    args.append(nc.dram_tensor("out_dram", _OUT[0], _mybir.dt.from_np(np.dtype(_OUT[1])), kind="ExternalOutput").ap())
    build(nc, *args)
    r = _run(nc, [arrays], core_ids=[0])
    return r.results[0]["out_dram"]
```
